# Optimizing a Trainium2 kernel written in Bass

```python
import numpy as np
import jax
import jax.numpy as jnp

def _softmax(x, axis=-1):
    return jax.nn.softmax(x, axis=axis)

def _gelu(x):
    return jax.nn.gelu(x, approximate=True)

def _silu(x):
    return jax.nn.silu(x)

def _sigmoid(x):
    return jax.nn.sigmoid(x)

def _layernorm(x, axis=-1, eps=1e-05):
    m = jnp.mean(x, axis=axis, keepdims=True)
    v = jnp.var(x, axis=axis, keepdims=True)
    return (x - m) / jnp.sqrt(v + eps)

def _scatter_add(tgt, idx, src, axis=0):
    return tgt.at[idx].add(src)

def _segment_sum(src, seg, n):
    return jax.ops.segment_sum(src, seg, n)
kernel_name = 'mk_dlrm_tower_d1_rec_r8_83852e'

def setup_inputs(seed: int=0):
    np.random.seed(seed)
    _w = jnp.asarray

    def _rec_inputs():
        import jax
        import jax.numpy as jnp
        _tk = jax.random.key(seed)
        dense_ctx = jax.random.normal(jax.random.fold_in(_tk, 190), (2048, 16), jnp.float32)
        ids = jnp.stack([jax.random.randint(jax.random.fold_in(_tk, 200 + f), (2048,), 0, v, jnp.int32) for f, v in enumerate([125000, 1000, 1250, 1000, 125000, 125000, 1250, 12500, 12500, 12500, 1000, 1250, 1000, 12500, 12500, 1250, 1000, 12500, 1250, 1000, 1000, 1000, 1250, 1000, 1000, 12500, 1250, 1000, 1000, 1000, 1000, 1000, 1000, 1000, 1250, 12500, 1000, 1000, 1000])], axis=1)
        tbl_0 = 0.05 * jax.random.normal(jax.random.fold_in(_tk, 500 + 0), (125000, 64), jnp.float32)
        tbl_1 = 0.05 * jax.random.normal(jax.random.fold_in(_tk, 500 + 1), (1000, 64), jnp.float32)
        tbl_2 = 0.05 * jax.random.normal(jax.random.fold_in(_tk, 500 + 2), (1250, 64), jnp.float32)
        tbl_3 = 0.05 * jax.random.normal(jax.random.fold_in(_tk, 500 + 3), (1000, 64), jnp.float32)
        tbl_4 = 0.05 * jax.random.normal(jax.random.fold_in(_tk, 500 + 4), (125000, 64), jnp.float32)
        tbl_5 = 0.05 * jax.random.normal(jax.random.fold_in(_tk, 500 + 5), (125000, 64), jnp.float32)
        tbl_6 = 0.05 * jax.random.normal(jax.random.fold_in(_tk, 500 + 6), (1250, 64), jnp.float32)
        tbl_7 = 0.05 * jax.random.normal(jax.random.fold_in(_tk, 500 + 7), (12500, 64), jnp.float32)
        tbl_8 = 0.05 * jax.random.normal(jax.random.fold_in(_tk, 500 + 8), (12500, 64), jnp.float32)
        tbl_9 = 0.05 * jax.random.normal(jax.random.fold_in(_tk, 500 + 9), (12500, 64), jnp.float32)
        tbl_10 = 0.05 * jax.random.normal(jax.random.fold_in(_tk, 500 + 10), (1000, 64), jnp.float32)
        tbl_11 = 0.05 * jax.random.normal(jax.random.fold_in(_tk, 500 + 11), (1250, 64), jnp.float32)
        tbl_12 = 0.05 * jax.random.normal(jax.random.fold_in(_tk, 500 + 12), (1000, 64), jnp.float32)
        tbl_13 = 0.05 * jax.random.normal(jax.random.fold_in(_tk, 500 + 13), (12500, 64), jnp.float32)
        tbl_14 = 0.05 * jax.random.normal(jax.random.fold_in(_tk, 500 + 14), (12500, 64), jnp.float32)
        tbl_15 = 0.05 * jax.random.normal(jax.random.fold_in(_tk, 500 + 15), (1250, 64), jnp.float32)
        tbl_16 = 0.05 * jax.random.normal(jax.random.fold_in(_tk, 500 + 16), (1000, 64), jnp.float32)
        tbl_17 = 0.05 * jax.random.normal(jax.random.fold_in(_tk, 500 + 17), (12500, 64), jnp.float32)
        tbl_18 = 0.05 * jax.random.normal(jax.random.fold_in(_tk, 500 + 18), (1250, 64), jnp.float32)
        tbl_19 = 0.05 * jax.random.normal(jax.random.fold_in(_tk, 500 + 19), (1000, 64), jnp.float32)
        tbl_20 = 0.05 * jax.random.normal(jax.random.fold_in(_tk, 500 + 20), (1000, 64), jnp.float32)
        tbl_21 = 0.05 * jax.random.normal(jax.random.fold_in(_tk, 500 + 21), (1000, 64), jnp.float32)
        tbl_22 = 0.05 * jax.random.normal(jax.random.fold_in(_tk, 500 + 22), (1250, 64), jnp.float32)
        tbl_23 = 0.05 * jax.random.normal(jax.random.fold_in(_tk, 500 + 23), (1000, 64), jnp.float32)
        tbl_24 = 0.05 * jax.random.normal(jax.random.fold_in(_tk, 500 + 24), (1000, 64), jnp.float32)
        tbl_25 = 0.05 * jax.random.normal(jax.random.fold_in(_tk, 500 + 25), (12500, 64), jnp.float32)
        tbl_26 = 0.05 * jax.random.normal(jax.random.fold_in(_tk, 500 + 26), (1250, 64), jnp.float32)
        tbl_27 = 0.05 * jax.random.normal(jax.random.fold_in(_tk, 500 + 27), (1000, 64), jnp.float32)
        tbl_28 = 0.05 * jax.random.normal(jax.random.fold_in(_tk, 500 + 28), (1000, 64), jnp.float32)
        tbl_29 = 0.05 * jax.random.normal(jax.random.fold_in(_tk, 500 + 29), (1000, 64), jnp.float32)
        tbl_30 = 0.05 * jax.random.normal(jax.random.fold_in(_tk, 500 + 30), (1000, 64), jnp.float32)
        tbl_31 = 0.05 * jax.random.normal(jax.random.fold_in(_tk, 500 + 31), (1000, 64), jnp.float32)
        tbl_32 = 0.05 * jax.random.normal(jax.random.fold_in(_tk, 500 + 32), (1000, 64), jnp.float32)
        tbl_33 = 0.05 * jax.random.normal(jax.random.fold_in(_tk, 500 + 33), (1000, 64), jnp.float32)
        tbl_34 = 0.05 * jax.random.normal(jax.random.fold_in(_tk, 500 + 34), (1250, 64), jnp.float32)
        tbl_35 = 0.05 * jax.random.normal(jax.random.fold_in(_tk, 500 + 35), (12500, 64), jnp.float32)
        tbl_36 = 0.05 * jax.random.normal(jax.random.fold_in(_tk, 500 + 36), (1000, 64), jnp.float32)
        tbl_37 = 0.05 * jax.random.normal(jax.random.fold_in(_tk, 500 + 37), (1000, 64), jnp.float32)
        tbl_38 = 0.05 * jax.random.normal(jax.random.fold_in(_tk, 500 + 38), (1000, 64), jnp.float32)
        _rk = jax.random.fold_in(_tk, 7)
        W_top1 = 0.0363456 * jax.random.normal(jax.random.fold_in(_tk, 801), (757, 512), jnp.float32)
        W_top2 = 0.0441942 * jax.random.normal(jax.random.fold_in(_tk, 802), (512, 256), jnp.float32)
        W_top3 = 0.0625 * jax.random.normal(jax.random.fold_in(_tk, 803), (256, 1), jnp.float32)
        b_top1 = jnp.zeros((512,), jnp.float32)
        b_top2 = jnp.zeros((256,), jnp.float32)
        return (dense_ctx, ids, tbl_0, tbl_1, tbl_2, tbl_3, tbl_4, tbl_5, tbl_6, tbl_7, tbl_8, tbl_9, tbl_10, tbl_11, tbl_12, tbl_13, tbl_14, tbl_15, tbl_16, tbl_17, tbl_18, tbl_19, tbl_20, tbl_21, tbl_22, tbl_23, tbl_24, tbl_25, tbl_26, tbl_27, tbl_28, tbl_29, tbl_30, tbl_31, tbl_32, tbl_33, tbl_34, tbl_35, tbl_36, tbl_37, tbl_38, W_top1, b_top1, W_top2, b_top2, W_top3)
    dense_ctx, ids, tbl_0, tbl_1, tbl_2, tbl_3, tbl_4, tbl_5, tbl_6, tbl_7, tbl_8, tbl_9, tbl_10, tbl_11, tbl_12, tbl_13, tbl_14, tbl_15, tbl_16, tbl_17, tbl_18, tbl_19, tbl_20, tbl_21, tbl_22, tbl_23, tbl_24, tbl_25, tbl_26, tbl_27, tbl_28, tbl_29, tbl_30, tbl_31, tbl_32, tbl_33, tbl_34, tbl_35, tbl_36, tbl_37, tbl_38, W_top1, b_top1, W_top2, b_top2, W_top3 = _rec_inputs()

    def _L0_rec_setup():
        import jax, jax.numpy as jnp
        import numpy as np
        NUM_FIELDS = 39
        _ROW, _COL = np.triu_indices(NUM_FIELDS, k=1)
        key = jax.random.key(seed)
        x = jax.random.normal(key, (2048, NUM_FIELDS, 64), dtype=jnp.float32)
        return {'x': x}
    _L0_rec_all = _L0_rec_setup()
    _L0_rec_in = {k: v for k, v in _L0_rec_all.items() if k in ()}
    del _L0_rec_all
    return {'dense_ctx': dense_ctx, 'ids': ids, 'tbl_0': tbl_0, 'tbl_1': tbl_1, 'tbl_2': tbl_2, 'tbl_3': tbl_3, 'tbl_4': tbl_4, 'tbl_5': tbl_5, 'tbl_6': tbl_6, 'tbl_7': tbl_7, 'tbl_8': tbl_8, 'tbl_9': tbl_9, 'tbl_10': tbl_10, 'tbl_11': tbl_11, 'tbl_12': tbl_12, 'tbl_13': tbl_13, 'tbl_14': tbl_14, 'tbl_15': tbl_15, 'tbl_16': tbl_16, 'tbl_17': tbl_17, 'tbl_18': tbl_18, 'tbl_19': tbl_19, 'tbl_20': tbl_20, 'tbl_21': tbl_21, 'tbl_22': tbl_22, 'tbl_23': tbl_23, 'tbl_24': tbl_24, 'tbl_25': tbl_25, 'tbl_26': tbl_26, 'tbl_27': tbl_27, 'tbl_28': tbl_28, 'tbl_29': tbl_29, 'tbl_30': tbl_30, 'tbl_31': tbl_31, 'tbl_32': tbl_32, 'tbl_33': tbl_33, 'tbl_34': tbl_34, 'tbl_35': tbl_35, 'tbl_36': tbl_36, 'tbl_37': tbl_37, 'tbl_38': tbl_38, 'W_top1': W_top1, 'b_top1': b_top1, 'W_top2': W_top2, 'b_top2': b_top2, 'W_top3': W_top3}

def reference(dense_ctx, ids, tbl_0, tbl_1, tbl_2, tbl_3, tbl_4, tbl_5, tbl_6, tbl_7, tbl_8, tbl_9, tbl_10, tbl_11, tbl_12, tbl_13, tbl_14, tbl_15, tbl_16, tbl_17, tbl_18, tbl_19, tbl_20, tbl_21, tbl_22, tbl_23, tbl_24, tbl_25, tbl_26, tbl_27, tbl_28, tbl_29, tbl_30, tbl_31, tbl_32, tbl_33, tbl_34, tbl_35, tbl_36, tbl_37, tbl_38, W_top1, b_top1, W_top2, b_top2, W_top3):
    import jax
    import jax.numpy as jnp

    def _L0_rec_ref(x):
        import jax, jax.numpy as jnp
        import numpy as np
        NUM_FIELDS = 39
        _ROW, _COL = np.triu_indices(NUM_FIELDS, k=1)
        s = jnp.sum(x, axis=-1)
        return s[:, _ROW] * s[:, _COL]
    e = jnp.stack([tbl_0[ids[:, 0]], tbl_1[ids[:, 1]], tbl_2[ids[:, 2]], tbl_3[ids[:, 3]], tbl_4[ids[:, 4]], tbl_5[ids[:, 5]], tbl_6[ids[:, 6]], tbl_7[ids[:, 7]], tbl_8[ids[:, 8]], tbl_9[ids[:, 9]], tbl_10[ids[:, 10]], tbl_11[ids[:, 11]], tbl_12[ids[:, 12]], tbl_13[ids[:, 13]], tbl_14[ids[:, 14]], tbl_15[ids[:, 15]], tbl_16[ids[:, 16]], tbl_17[ids[:, 17]], tbl_18[ids[:, 18]], tbl_19[ids[:, 19]], tbl_20[ids[:, 20]], tbl_21[ids[:, 21]], tbl_22[ids[:, 22]], tbl_23[ids[:, 23]], tbl_24[ids[:, 24]], tbl_25[ids[:, 25]], tbl_26[ids[:, 26]], tbl_27[ids[:, 27]], tbl_28[ids[:, 28]], tbl_29[ids[:, 29]], tbl_30[ids[:, 30]], tbl_31[ids[:, 31]], tbl_32[ids[:, 32]], tbl_33[ids[:, 33]], tbl_34[ids[:, 34]], tbl_35[ids[:, 35]], tbl_36[ids[:, 36]], tbl_37[ids[:, 37]], tbl_38[ids[:, 38]]], axis=1)
    z = _L0_rec_ref(e)
    z = z.reshape(z.shape[0], -1)
    h = jnp.concatenate([z, dense_ctx], axis=1)
    h = jnp.maximum(h @ W_top1 + b_top1, 0.0)
    h = jnp.maximum(h @ W_top2 + b_top2, 0.0)
    y = h @ W_top3
    return y

_drawn_inputs = setup_inputs


def setup_inputs(seed=0):
    import zlib

    import numpy as np

    out = dict(_drawn_inputs(seed))
    spreads = {'b_top1': (0.0, 0.1), 'b_top2': (0.0, 0.1)}
    factors = {}
    for name, (base, spread) in spreads.items():
        noise = np.random.default_rng([zlib.crc32(name.encode()), seed]).standard_normal(out[name].shape)
        drawn = base * np.exp(spread * noise) if base else spread * noise
        out[name] = jnp.asarray(drawn.astype(out[name].dtype))
    for name, factor in factors.items():
        out[name] = (out[name] * factor).astype(out[name].dtype)
    return out
```

```python
from contextlib import ExitStack

import concourse.bass as bass
from concourse import mybir

ALU = mybir.AluOpType
ACT = mybir.ActivationFunctionType
AX = mybir.AxisListType
F32 = mybir.dt.float32
BF16 = mybir.dt.bfloat16
I32 = mybir.dt.int32

P = 128
BATCH = 2048
CHUNK = 512
CHUNKS = BATCH // CHUNK
TILES = CHUNK // P
DIM = 64
FIELDS = 39
DENSE = 16

VOCAB = [125000, 1000, 1250, 1000, 125000, 125000, 1250, 12500, 12500, 12500, 1000, 1250, 1000, 12500, 12500,
         1250, 1000, 12500, 1250, 1000, 1000, 1000, 1250, 1000, 1000, 12500, 1250, 1000, 1000, 1000, 1000,
         1000, 1000, 1000, 1250, 12500, 1000, 1000, 1000]

SHELVES = 125
SPLIT = 112
F8 = [f for f in range(FIELDS) if VOCAB[f] == SHELVES * 8]
F10 = [f for f in range(FIELDS) if VOCAB[f] == SHELVES * 10]
ONCHIP = F8 + F10
FETCHED = [f for f in range(FIELDS) if f not in ONCHIP]
ORDER = ONCHIP + FETCHED
NON, NF = len(ONCHIP), len(FETCHED)
LANE = 32
PER_GROUP = P // LANE
GROUPS = NON // PER_GROUP
GROUP_W = [8 if ORDER[g * PER_GROUP] in F8 else 10 for g in range(GROUPS)]
PARTS = 3
SROWS = PARTS * FIELDS

PAIRS = FIELDS * (FIELDS - 1) // 2
K1 = PAIRS + DENSE
KCH = -(-K1 // P)
KLAST = K1 - (KCH - 1) * P
ZLAST = PAIRS - (KCH - 1) * P
H1, H2 = 512, 256
M1, M2 = H1 // P, H2 // P
FIRST = 0
ROUND = 12582912.0

QR_ROWS = NON * CHUNKS

C_PART, C_J8, C_J10, C_INV, C_OFF, C_NEGW = range(6)
O_SUM = 0
O_ROW = O_SUM + GROUPS * SROWS
O_COL = O_ROW + PAIRS
O_ID = O_COL + PAIRS
NCONST = O_ID + P


def build_tower(nc, ids_rows, ids_cols, dense_t, tab8, tab10, big, w1, w2, columns, fconst, bconst, out):
    assert K1 == w1.shape[0] and QR_ROWS <= P and SROWS <= P
    with ExitStack() as ctx:
        def sb(name, shape, dt):
            return ctx.enter_context(nc.sbuf_tensor(name, shape, dt))

        def ps(name, shape):
            return ctx.enter_context(nc.psum_tensor(name, shape, F32))

        def sem(name):
            return ctx.enter_context(nc.semaphore(name))

        shelf_dram = nc.dram_tensor("shelf_scratch", (CHUNKS, NON, CHUNK), BF16, kind="Internal").ap()
        slot_dram = nc.dram_tensor("slot_scratch", (CHUNKS, NON, CHUNK), BF16, kind="Internal").ap()

        fc = sb("fc", [P, 6], F32)
        bc = sb("bc", [P, NCONST], BF16)
        idr = sb("idr", [QR_ROWS, CHUNK], I32)
        shelf_f = sb("shelf_f", [QR_ROWS, CHUNK], F32)
        shelf_h = sb("shelf_h", [QR_ROWS, CHUNK], BF16)
        slot_h = sb("slot_h", [QR_ROWS, CHUNK], BF16)
        idc = sb("idc", [P, CHUNKS * TILES * NF], I32)
        idx = sb("idx", [P, TILES, NF], I32)
        stage = sb("stage", [P, 4, PER_GROUP * 10 * DIM], F32)
        tsum = sb("tsum", [P, GROUPS, PER_GROUP * 10], F32)
        trest = sb("trest", [P, GROUPS, PER_GROUP * 10], F32)
        tparts = sb("tparts", [P, NON, LANE], BF16)
        shelf_b = sb("shelf_b", [P, NON, CHUNK], BF16)
        slot_b = sb("slot_b", [P, GROUPS, CHUNK], BF16)
        onehot = sb("onehot", [P, NON, CHUNK], BF16)
        picked = sb("picked", [P, GROUPS, CHUNK], BF16)
        rows = sb("rows", [P, TILES, NF, DIM], F32)
        rsum = sb("rsum", [P, TILES, NF], F32)
        rrest = sb("rrest", [P, 2, TILES, NF], F32)
        rparts = sb("rparts", [P, TILES, PARTS, FIELDS], BF16)
        s_t = sb("s_t", [SROWS, CHUNK], BF16)
        z = sb("z", [P, KCH - 1, CHUNK], F32)
        zlast = sb("zlast", [KLAST, BATCH], F32)
        zrow = sb("zrow", [P, CHUNK], F32)
        w1_sb = sb("w1_sb", [P, KCH, H1], F32)
        w2_sb = sb("w2_sb", [P, M1, H2], F32)
        cols = sb("cols", [P, 2 * M2 + M1], F32)
        w3_sb, b1_sb, b2_sb = cols[:, 0:M2], cols[:, M2:M2 + M1], cols[:, M2 + M1:]
        h1 = sb("h1", [P, M1, CHUNK], F32)
        h2 = sb("h2", [P, M2, CHUNK], F32)
        y_sb = sb("y_sb", [1, BATCH], F32)

        pg = [ps(f"pg{i}", [P, CHUNK]) for i in range(2)]
        psum_s = ps("psum_s", [P, CHUNK])
        pa = ps("pa", [P, CHUNK])
        pb = ps("pb", [P, CHUNK])
        ph = [ps(f"ph{i}", [P, CHUNK]) for i in range(2)]
        py = ps("py", [1, CHUNK])

        sum_w = bc[:, O_SUM:O_ROW].rearrange("p (g s) -> p g s", g=GROUPS)
        ident = bc[:, O_ID:O_ID + P]

        ids_in = sem("ids_in")
        consts_in = sem("consts_in")
        bconst_in = sem("bconst_in")
        idc_in = sem("idc_in")
        dense_in = sem("dense_in")
        weights_in = sem("weights_in")
        table_in = [sem(f"table_in{i}") for i in range(4)]
        shelf_calc = sem("shelf_calc")
        shelf_ready = sem("shelf_ready")
        slot_ready = sem("slot_ready")
        scratch_shelf = sem("scratch_shelf")
        scratch_slot = sem("scratch_slot")
        shelf_in = [sem(f"shelf_in{g}") for g in range(GROUPS)]
        slot_in = sem("slot_in")
        zeroed = sem("zeroed")
        tables_summed = sem("tables_summed")
        table_split = sem("table_split")
        tparts_ready = sem("tparts_ready")
        onehot_ready = sem("onehot_ready")
        looked_up = sem("looked_up")
        picked_ready = sem("picked_ready")
        idx_ready = sem("idx_ready")
        rows_in = [sem(f"rows_in{t}") for t in range(TILES)]
        rows_free = [sem(f"rows_free{t}") for t in range(TILES)]
        row_split = sem("row_split")
        rparts_ready = sem("rparts_ready")
        s_acc = sem("s_acc")
        s_ready = sem("s_ready")
        selected = sem("selected")
        first_copied = sem("first_copied")
        z_ready = sem("z_ready")
        h1_acc = sem("h1_acc")
        h1_ready = sem("h1_ready")
        h2_acc = sem("h2_acc")
        h2_ready = sem("h2_ready")
        y_acc = sem("y_acc")
        y_ready = sem("y_ready")
        y_out = sem("y_out")


        block = ctx.enter_context(nc.Block())

        @block.sync
        def _(sp):
            sp.dma_start(idr[:, :], ids_rows).then_inc(ids_in, 16)
            sp.dma_start(fc[:, :], fconst).then_inc(consts_in, 16)

            def load_table(g):
                n = PER_GROUP * GROUP_W[g] * DIM
                src = tab8 if GROUP_W[g] == 8 else tab10
                at = n * (g if GROUP_W[g] == 8 else g - len(F8) // PER_GROUP)
                if g >= 4:
                    sp.wait_ge(tables_summed, g - 3)
                for a, b in ((0, SPLIT), (SPLIT, SHELVES)):
                    sp.dma_start(stage[a:b, g % 4, 0:n], src[a:b, at:at + n]).then_inc(table_in[g % 4], 16)

            load_table(0)
            load_table(1)
            sp.wait_ge(shelf_ready, 1)
            sp.dma_start(shelf_dram.rearrange("c f n -> (c f) n"), shelf_h[:, :]).then_inc(scratch_shelf, 16)
            sp.wait_ge(slot_ready, 1)
            sp.dma_start(slot_dram.rearrange("c f n -> (c f) n"), slot_h[:, :]).then_inc(scratch_slot, 16)
            load_table(2)
            load_table(3)
            sp.wait_ge(scratch_shelf, 16)
            sp.wait_ge(scratch_slot, 16)

            def load_ids(c):
                for g in range(GROUPS):
                    sp.dma_start(shelf_b[:, g * PER_GROUP:(g + 1) * PER_GROUP, :],
                                 shelf_dram[bass.ds(c, 1), g * PER_GROUP:(g + 1) * PER_GROUP, :]
                                 .rearrange("c f n -> c (f n)").partition_broadcast(P)).then_inc(shelf_in[g], 16)
                for lane in range(PER_GROUP):
                    sp.dma_start(slot_b[lane * LANE:(lane + 1) * LANE, :, :],
                                 slot_dram[bass.ds(c, 1), :, :]
                                 .rearrange("c (g l) n -> l c g n", l=PER_GROUP)[lane]
                                 .partition_broadcast(LANE)).then_inc(slot_in, 16)

            load_ids(0)
            for g in range(4, GROUPS):
                load_table(g)
            with sp.Fori(1, CHUNKS) as c:
                sp.wait_ge(onehot_ready, c * GROUPS)
                sp.wait_ge(picked_ready, c * GROUPS)
                load_ids(c)
            sp.wait_ge(y_ready, CHUNKS)
            sp.dma_start(out, y_sb[:, :]).then_inc(y_out, 16)
            sp.wait_ge(y_out, 16)

        @block.gpsimd
        def _(pool):
            pool.dma_start(idc[:, :], ids_cols).then_inc(idc_in, 16)
            pool.wait_ge(idc_in, 16)

            def fetch(c):
                for t in range(TILES):
                    if c is not FIRST:
                        pool.wait_ge(rows_free[t], c)
                    pool.tensor_copy(idx[:, t, :], idc[:, bass.ds(c * (TILES * NF) + t * NF, NF)]
                                     ).then_inc(idx_ready, 1)
                    pool.wait_ge(idx_ready, c * TILES + t + 1)
                    pool.nop(nofuse=True)
                    for k in range(NF):
                        pool.indirect_dma_start(rows[:, t, k, :], None, big[k],
                                                bass.IndirectOffsetOnAxis(ap=idx[:, t, k:k + 1], axis=0)
                                                ).then_inc(rows_in[t], 16)

            fetch(FIRST)
            with pool.Fori(1, CHUNKS) as c:
                fetch(c)

        @block.vector
        def _(dve):
            dve.wait_ge(ids_in, 16)
            dve.wait_ge(consts_in, 16)
            dve.tensor_scalar(shelf_f[:, :], idr[:, :], fc[0:QR_ROWS, C_INV:C_INV + 1],
                              fc[0:QR_ROWS, C_OFF:C_OFF + 1], ALU.mult, ALU.add).then_inc(shelf_calc, 1)
            dve.wait_ge(shelf_calc, 1)
            dve.tensor_scalar(shelf_h[:, :], shelf_f[:, :], ROUND, ROUND, ALU.add,
                              ALU.subtract).then_inc(shelf_ready, 1)
            dve.wait_ge(shelf_ready, 1)
            dve.scalar_tensor_tensor(out=slot_h[:, :], in0=shelf_h[:, :], scalar=fc[0:QR_ROWS, C_NEGW:C_NEGW + 1],
                                     in1=idr[:, :], op0=ALU.mult, op1=ALU.add).then_inc(slot_ready, 1)
            dve.memset(tparts[:, :, :], 0.0).then_inc(zeroed, 1)
            dve.memset(rparts[:, :, :, :], 0.0).then_inc(zeroed, 1)

            def split(value, rest, part, calc, base, done):
                dve.tensor_copy(part(0), value).then_inc(calc, 1)
                dve.wait_ge(calc, base + 1)
                dve.tensor_tensor(rest(0), value, part(0), ALU.subtract).then_inc(calc, 1)
                dve.wait_ge(calc, base + 2)
                dve.tensor_copy(part(1), rest(0)).then_inc(calc, 1)
                dve.wait_ge(calc, base + 3)
                dve.tensor_tensor(rest(1), rest(0), part(1), ALU.subtract).then_inc(calc, 1)
                dve.wait_ge(calc, base + 4)
                dve.tensor_copy(part(2), rest(1)).then_inc(done, 1)

            def table_sums(g):
                w = GROUP_W[g]
                dve.wait_ge(table_in[g % 4], 32 * (g // 4 + 1))
                if g == 0:
                    dve.wait_ge(zeroed, 2)
                dve.tensor_reduce(tsum[0:SHELVES, g, 0:PER_GROUP * w],
                                  stage[0:SHELVES, g % 4, 0:PER_GROUP * w * DIM].rearrange("p (r d) -> p r d", d=DIM),
                                  AX.X, ALU.add).then_inc(tables_summed, 1)
                dve.wait_ge(tables_summed, g + 1)

                def v(x):
                    return x[0:SHELVES, g, 0:PER_GROUP * w].rearrange("p (f j) -> p f j", j=w)

                split(v(tsum), lambda i: v(trest) if i == 0 else v(tsum),
                      lambda i: tparts[0:SHELVES, g * PER_GROUP:(g + 1) * PER_GROUP, i * w:(i + 1) * w],
                      table_split, 4 * g, tparts_ready)

            def onehots(c, g):
                dve.wait_ge(shelf_in[g], 16 * (c + 1))
                for f in range(g * PER_GROUP, (g + 1) * PER_GROUP):
                    last = dve.tensor_scalar(onehot[0:SHELVES, f, :], shelf_b[0:SHELVES, f, :],
                                             fc[0:SHELVES, C_PART:C_PART + 1], None, ALU.is_equal)
                last.then_inc(onehot_ready, 1)

            for g in range(4):
                table_sums(g)
            for g in range(GROUPS):
                onehots(0, g)
            for g in range(4, GROUPS):
                table_sums(g)

            def lookups(c):
                dve.wait_ge(slot_in, 16 * PER_GROUP * (c + 1))
                for g in range(GROUPS):
                    dve.wait_ge(looked_up, c * GROUPS + g + 1)
                    j = C_J8 if GROUP_W[g] == 8 else C_J10
                    dve.scalar_tensor_tensor(out=picked[:, g, :], in0=slot_b[:, g, :], scalar=fc[:, j:j + 1],
                                             in1=pg[g % 2][:, :], op0=ALU.is_equal,
                                             op1=ALU.mult).then_inc(picked_ready, 1)

            def fetched(c):
                for t in range(TILES):
                    dve.wait_ge(rows_in[t], 16 * NF * (c + 1))
                    dve.tensor_reduce(rsum[:, t, :], rows[:, t, :, :], AX.X, ALU.add).then_inc(rows_free[t], 1)
                for t in range(TILES):
                    dve.wait_ge(rows_free[t], c + 1)
                split(rsum[:, :, :], lambda i: rrest[:, i, :, :], lambda i: rparts[:, :, i, NON:FIELDS],
                      row_split, 4 * c, rparts_ready)

            def pairs(c):
                for k in range(KCH):
                    dve.wait_ge(selected, c * KCH + k + 1)
                    dve.wait_ge(first_copied, c * KCH + k + 1)
                    n = P if k < KCH - 1 else ZLAST
                    o = z[:, k, :] if k < KCH - 1 else zlast[0:n, bass.ds(c * CHUNK, CHUNK)]
                    dve.tensor_tensor(o, zrow[0:n, :], pb[0:n, :], ALU.mult).then_inc(z_ready, 1)

            with dve.Fori(0, CHUNKS - 1) as c:
                lookups(c)
                fetched(c)
                pairs(c)
                for g in range(GROUPS):
                    onehots(c + 1, g)
            lookups(CHUNKS - 1)
            fetched(CHUNKS - 1)
            pairs(CHUNKS - 1)

        @block.scalar
        def _(act):
            act.dma_start(bc[:, :], bconst).then_inc(bconst_in, 16)
            act.dma_start(zlast[ZLAST:KLAST, :], dense_t).then_inc(dense_in, 16)
            act.dma_start(w1_sb[:, 0:KCH - 1, :], w1[0:(KCH - 1) * P, :].rearrange("(k p) n -> p k n", p=P)
                          ).then_inc(weights_in, 16)
            act.dma_start(w1_sb[0:KLAST, KCH - 1, :], w1[(KCH - 1) * P:K1, :]).then_inc(weights_in, 16)
            act.dma_start(w2_sb[:, :, :], w2.rearrange("(k p) n -> p k n", p=P)).then_inc(weights_in, 16)
            act.dma_start(cols[:, :], columns).then_inc(weights_in, 16)
            act.wait_ge(weights_in, 64)
            with act.Fori(0, CHUNKS) as c:
                act.wait_ge(s_acc, c + 1)
                act.copy(s_t[:, :], psum_s[0:SROWS, :]).then_inc(s_ready, 1)
                for k in range(KCH):
                    n = P if k < KCH - 1 else ZLAST
                    act.wait_ge(selected, c * KCH + k + 1)
                    if k > 0:
                        act.wait_ge(z_ready, c * KCH + k)
                    act.copy(zrow[0:n, :], pa[0:n, :]).then_inc(first_copied, 1)
                for m in range(M1):
                    act.wait_ge(h1_acc, c * M1 + m + 1)
                    act.activation(h1[:, m, :], ph[m % 2][:, :], ACT.Relu,
                                   bias=b1_sb[:, m:m + 1]).then_inc(h1_ready, 1)
                for m in range(M2):
                    act.wait_ge(h2_acc, c * M2 + m + 1)
                    act.activation(h2[:, m, :], (pa if m == 0 else pb)[:, :], ACT.Relu,
                                   bias=b2_sb[:, m:m + 1]).then_inc(h2_ready, 1)
                act.wait_ge(y_acc, c + 1)
                act.copy(y_sb[:, bass.ds(c * CHUNK, CHUNK)], py[:, :]).then_inc(y_ready, 1)

        @block.tensor
        def _(pe):
            pe.wait_ge(bconst_in, 16)
            pe.wait_ge(weights_in, 64)
            pe.wait_ge(dense_in, 16)

            def lookup(c, g):
                pe.wait_ge(tparts_ready, g + 1)
                pe.wait_ge(onehot_ready, c * GROUPS + g + 1)
                if g >= 2:
                    pe.wait_ge(picked_ready, c * GROUPS + g - 1)
                for lane in range(PER_GROUP):
                    f = g * PER_GROUP + lane
                    last = pe.matmul(pg[g % 2][lane * LANE:(lane + 1) * LANE, :], tparts[0:SHELVES, f, :],
                                     onehot[0:SHELVES, f, :], start=True, stop=True)
                last.then_inc(looked_up, 1)

            def gather_sum(c, g):
                pe.wait_ge(picked_ready, c * GROUPS + g + 1)
                pe.matmul(psum_s[0:SROWS, :], sum_w[:, g, :], picked[:, g, :], start=(g == 0), stop=False,
                          skip_group_check=True)

            with pe.Fori(0, CHUNKS) as c:
                for g in range(GROUPS):
                    lookup(c, g)
                    if g > 0:
                        gather_sum(c, g - 1)
                gather_sum(c, GROUPS - 1)
                pe.wait_ge(rparts_ready, c + 1)
                for t in range(TILES):
                    last = pe.matmul(psum_s[0:SROWS, t * P:(t + 1) * P],
                                     rparts[:, t, :, :].rearrange("p a f -> p (a f)"), ident,
                                     start=False, stop=True, skip_group_check=True)
                last.then_inc(s_acc, 1)

                def select(k):
                    n = P if k < KCH - 1 else ZLAST
                    if k == 0:
                        pe.wait_ge(s_ready, c + 1)
                    else:
                        pe.wait_ge(z_ready, c * KCH + k)
                    a = O_ROW + k * P
                    pe.matmul(pa[0:n, :], bc[0:SROWS, a:a + n], s_t[:, :], start=True, stop=True)
                    a = O_COL + k * P
                    pe.matmul(pb[0:n, :], bc[0:SROWS, a:a + n], s_t[:, :], start=True,
                              stop=True).then_inc(selected, 1)

                def layer1(k, m):
                    n = P if k < KCH - 1 else KLAST
                    zk = z[:, k, :] if k < KCH - 1 else zlast[:, bass.ds(c * CHUNK, CHUNK)]
                    return pe.matmul(ph[m % 2][:, :], w1_sb[0:n, k, m * P:(m + 1) * P], zk,
                                     start=(k == 0), stop=(k == KCH - 1))

                select(0)
                for k in range(KCH):
                    if k + 1 < KCH:
                        select(k + 1)
                    else:
                        pe.wait_ge(z_ready, c * KCH + KCH)
                    for m in range(2):
                        mm = layer1(k, m)
                        if k == KCH - 1:
                            mm.then_inc(h1_acc, 1)
                for m in range(2, M1):
                    pe.wait_ge(h1_ready, c * M1 + m - 1)
                    for k in range(KCH):
                        mm = layer1(k, m)
                    mm.then_inc(h1_acc, 1)
                for k in range(M1):
                    pe.wait_ge(h1_ready, c * M1 + k + 1)
                    for m in range(M2):
                        mm = pe.matmul((pa if m == 0 else pb)[:, :], w2_sb[:, k, m * P:(m + 1) * P], h1[:, k, :],
                                       start=(k == 0), stop=(k == M1 - 1))
                        if k == M1 - 1:
                            mm.then_inc(h2_acc, 1)
                for m in range(M2):
                    pe.wait_ge(h2_ready, c * M2 + m + 1)
                    mm = pe.matmul(py[:, :], w3_sb[:, m:m + 1], h2[:, m, :], start=(m == 0), stop=(m == M2 - 1))
                mm.then_inc(y_acc, 1)


def _shape_constants(np):
    fconst = np.zeros((P, 6), np.float32)
    p = np.arange(P)
    fconst[:, C_PART] = p
    for col, w in ((C_J8, 8), (C_J10, 10)):
        r = p % LANE
        fconst[:, col] = np.where(r < PARTS * w, r % w, -1)
    for row in range(QR_ROWS):
        w = VOCAB[ORDER[row % NON]] // SHELVES
        fconst[row, C_INV] = 1.0 / w
        fconst[row, C_OFF] = 0.5 / w - 0.5
        fconst[row, C_NEGW] = -w
    bconst = np.zeros((P, NCONST), np.float32)
    for g in range(GROUPS):
        w = GROUP_W[g]
        for lane in range(PER_GROUP):
            for i in range(PARTS):
                a = lane * LANE + i * w
                bconst[a:a + w, O_SUM + g * SROWS + i * FIELDS + g * PER_GROUP + lane] = 1
    first, second = np.triu_indices(FIELDS, k=1)
    place = np.argsort(np.array(ORDER))
    for i in range(PARTS):
        bconst[i * FIELDS + place[first], O_ROW + np.arange(PAIRS)] = 1
        bconst[i * FIELDS + place[second], O_COL + np.arange(PAIRS)] = 1
    bconst[p, O_ID + p] = 1
    return fconst, bconst


def kernel(**inputs):
    import numpy as np
    import concourse.bacc as bacc
    from concourse.bass_utils import run_bass_kernel_spmd

    nc = bacc.Bacc("TRN2", target_bir_lowering=False, num_devices=1)
    arrays = {}

    def dram(name, a):
        a = np.ascontiguousarray(a)
        arrays[name] = a
        return nc.dram_tensor(name, a.shape, mybir.dt.from_np(a.dtype), kind="ExternalInput").ap()

    ids = np.asarray(inputs["ids"])
    on_chip = ids.T[np.array(ONCHIP)].reshape(NON, CHUNKS, CHUNK).transpose(1, 0, 2).reshape(QR_ROWS, CHUNK)
    by_row = ids[:, np.array(FETCHED)].reshape(BATCH // P, P, NF).transpose(1, 0, 2).reshape(P, -1)

    def shelves(fields):
        return np.concatenate([np.asarray(inputs[f"tbl_{f}"]).reshape(SHELVES, -1) for f in fields], axis=1)

    columns = np.concatenate([np.asarray(inputs[n]).reshape(-1, P).T for n in ("W_top3", "b_top1", "b_top2")], axis=1)
    fconst, bconst = _shape_constants(np)
    out = nc.dram_tensor("out", (1, BATCH), F32, kind="ExternalOutput").ap()
    build_tower(
        nc, dram("ids_rows", on_chip), dram("ids_cols", by_row), dram("dense_t", np.asarray(inputs["dense_ctx"]).T),
        dram("tab8", shelves(F8)), dram("tab10", shelves(F10)),
        [dram(f"tab_{f}", inputs[f"tbl_{f}"]) for f in FETCHED],
        dram("w1", inputs["W_top1"]), dram("w2", inputs["W_top2"]), dram("columns", columns),
        dram("fconst", fconst), dram("bconst", bconst.astype(np.dtype("bfloat16"))), out)
    r = run_bass_kernel_spmd(nc, [arrays], core_ids=[0])
    return r.results[0]["out"].reshape(BATCH, 1)
```

```python
from contextlib import ExitStack

import concourse.bass as bass
from concourse import mybir

ALU = mybir.AluOpType
ACT = mybir.ActivationFunctionType
AX = mybir.AxisListType
F32 = mybir.dt.float32
BF16 = mybir.dt.bfloat16
F32R = mybir.dt.float32r
I32 = mybir.dt.int32
FIRST = 0

P = 128
BATCH = 2048
CHUNK = 512
CHUNKS = BATCH // CHUNK
TILES = CHUNK // P
DIM = 64
FIELDS = 39
DENSE = 16

VOCAB = [125000, 1000, 1250, 1000, 125000, 125000, 1250, 12500, 12500, 12500, 1000, 1250, 1000, 12500, 12500,
         1250, 1000, 12500, 1250, 1000, 1000, 1000, 1250, 1000, 1000, 12500, 1250, 1000, 1000, 1000, 1000,
         1000, 1000, 1000, 1250, 12500, 1000, 1000, 1000]

SHELVES = 125
SPLIT = 112
W8, W10, WMID = 8, 10, 100
F8 = [f for f in range(FIELDS) if VOCAB[f] == SHELVES * W8]
F10 = [f for f in range(FIELDS) if VOCAB[f] == SHELVES * W10]
EARLY = F8 + F10
LARGE = [f for f in range(FIELDS) if VOCAB[f] > SHELVES * WMID]
MIDDLE = [f for f in range(FIELDS) if VOCAB[f] == SHELVES * WMID]
NMID = 2
LATE = LARGE + MIDDLE
ORDER = EARLY + LATE
NE, NL = len(EARLY), len(LATE)
NFETCH = NL - NMID
NHOT = NE + NMID

LANE = 32
PER_GROUP = P // LANE
GROUPS = NE // PER_GROUP
GROUP_W = [W8 if ORDER[g * PER_GROUP] in F8 else W10 for g in range(GROUPS)]
G8 = GROUP_W.count(W8)
BATCHES = [(0, 3), (3, G8), (G8, GROUPS)]
PARTS = 3
RE, RL = PARTS * NE, PARTS * NL
PIECE = 25
PIECES = WMID // PIECE
STAGES = 4

PAIRS = FIELDS * (FIELDS - 1) // 2
EARLY_PAIRS = NE * (NE - 1) // 2
KCH = 6
KROWS = [P, P, EARLY_PAIRS - 2 * P, P, P, PAIRS - EARLY_PAIRS + DENSE - 2 * P]
H1, H2 = 512, 256
M1, M2 = H1 // P, H2 // P
ROUND = 12582912.0
QR_ROWS = CHUNKS * NHOT

C_PART, C_J8, C_J10, C_INV, C_OFF, C_NEGW = range(6)
O_SUM = 0
O_E1 = O_SUM + GROUPS * RE
O_E2 = O_E1 + KCH * P
O_L1 = O_E2 + 3 * P
O_L2 = O_L1 + P
O_ID = O_L2 + 3 * P
O_SLOT = O_ID + P
NCONST = O_SLOT + WMID

MID_TILES = min(TILES, CHUNK // (NMID * WMID))
MID_STEPS = {1: [0], 2: [0, 2], 4: [0, 2, 4, 6]}[TILES // MID_TILES]
GROUP_STEPS = [7, 9, 11, 13, 15, 17, 19]
SUM_STEPS = GROUP_STEPS[1:] + [21]
ROW_STEPS = {2: 2, 3: 3}
NEXT_ROW_STEPS = {0: 15, 1: 23}
HOT_STEPS = {3: 10, 4: 12, 5: 14, 6: 16}
AHEAD = 3
PIECE_STEPS = [12, 15, 18, 20, 22]
ZRING = 3


def build_tower(nc, ids_rows, ids_cols, dense_t, tab8, tab10, late_tables, w1, w2, columns, fconst, bconst, out):
    assert EARLY_PAIRS <= 3 * P and sum(KROWS) == w1.shape[0] and QR_ROWS <= P
    with ExitStack() as ctx:
        def sb(name, shape, dt):
            return ctx.enter_context(nc.sbuf_tensor(name, shape, dt))

        def ps(name):
            return ctx.enter_context(nc.psum_tensor(name, [P, CHUNK], F32))

        def sem(name):
            return ctx.enter_context(nc.semaphore(name))

        shelf_dram = nc.dram_tensor("shelf_scratch", (CHUNKS, NHOT, CHUNK), BF16, kind="Internal").ap()
        slot_dram = nc.dram_tensor("slot_scratch", (CHUNKS, NHOT, CHUNK), BF16, kind="Internal").ap()

        fc = sb("fc", [P, 6], F32)
        bc = sb("bc", [P, NCONST], BF16)
        shelf_h = sb("shelf_h", [QR_ROWS, CHUNK], BF16)
        slot_h = sb("slot_h", [QR_ROWS, CHUNK], BF16)
        idc = sb("idc", [P, CHUNKS * TILES * NL], I32)
        idx = sb("idx", [P, TILES, NL], I32)
        mid_shelf = sb("mid_shelf", [P, CHUNKS * TILES, NMID], F32)
        mid_slot = sb("mid_slot", [P, CHUNKS * TILES * NMID], F32)
        stage = sb("stage", [P, STAGES, PER_GROUP * W10 * DIM], F32)
        tsum = sb("tsum", [P, NE, W10], F32)
        trest = sb("trest", [P, NE, W10], F32)
        tparts = sb("tparts", [P, NE, LANE], BF16)
        msum = sb("msum", [P, NMID, WMID], F32)
        mrest = sb("mrest", [P, NMID, WMID], F32)
        mparts = sb("mparts", [P, NMID, PARTS, WMID], BF16)
        shelf_b = sb("shelf_b", [P, NHOT, CHUNK], BF16)
        slot_b = sb("slot_b", [P, GROUPS, CHUNK], BF16)
        onehot = sb("onehot", [P, NHOT, CHUNK], BF16)
        picked = sb("picked", [P, GROUPS, CHUNK], BF16)
        mid_picked = sb("mid_picked", [P, MID_TILES * NMID, WMID], F32)
        rows = sb("rows", [P, TILES, NL, DIM], F32)
        rsum = sb("rsum", [P, TILES, NL], F32)
        rrest = sb("rrest", [P, 2, TILES, NL], F32)
        rparts = sb("rparts", [P, TILES, PARTS, NL], BF16)
        s_early = sb("s_early", [RE, CHUNK], BF16)
        s_late = sb("s_late", [RL, CHUNK], BF16)
        factor = sb("factor", [P, CHUNK], F32)
        z = sb("z", [P, CHUNK], F32)
        idr = factor[0:QR_ROWS, :].bitcast(I32)
        shelf_f = z[0:QR_ROWS, :]
        z_hi = sb("z_hi", [P, ZRING, CHUNK], F32R)
        z_lo = sb("z_lo", [P, ZRING, CHUNK], F32R)
        dense = sb("dense", [DENSE, CHUNK], F32)
        w1_hi = sb("w1_hi", [P, KCH, H1], F32R)
        w1_lo = sb("w1_lo", [P, KCH, H1], F32R)
        w2_sb = sb("w2_sb", [P, M1, H2], F32)
        cols = sb("cols", [P, 2 * M2 + M1], F32)
        w3_sb, b1_sb, b2_sb = cols[:, 0:M2], cols[:, M2:M2 + M1], cols[:, M2 + M1:]
        hidden = sb("hidden", [P, M1 + M2, CHUNK], F32)
        w1_raw = hidden
        h1, h2 = hidden[:, 0:M1, :], hidden[:, M1:, :]
        y_sb = sb("y_sb", [1, CHUNK], F32)

        look = ps("look")
        early = ps("early")
        pa = ps("pa")
        pb = ps("pb")
        ph = [ps(f"ph{m}") for m in range(M1)]

        FIRST_BANKS = [look, ph[3]]
        SPREAD_BANKS = ph[0:3]
        sum_w = bc[:, O_SUM:O_E1].rearrange("p (g s) -> p g s", g=GROUPS)
        ident = bc[:, O_ID:O_ID + P]
        slots = bc[:, O_SLOT:NCONST]

        ids_in = sem("ids_in")
        consts_in = sem("consts_in")
        bconst_in = sem("bconst_in")
        select_in = sem("select_in")
        idc_in = sem("idc_in")
        dense_in = sem("dense_in")
        w1_in = sem("w1_in")
        w2_in = sem("w2_in")
        w1_rounded = sem("w1_rounded")
        w1_split = sem("w1_split")
        stage_in = [sem(f"stage_in{i}") for i in range(STAGES)]
        stage_summed = sem("stage_summed")
        shelf_calc = sem("shelf_calc")
        shelf_spread = sem("shelf_spread")
        shelf_copied = sem("shelf_copied")
        shelf_ready = sem("shelf_ready")
        slot_ready = sem("slot_ready")
        mid_calc = sem("mid_calc")
        scratch_shelf = sem("scratch_shelf")
        scratch_slot = sem("scratch_slot")
        shelf_in = [sem(f"shelf_in{g}") for g in range(GROUPS + 1)]
        slot_in = [sem(f"slot_in{n}") for n in range(PER_GROUP)]
        zeroed = sem("zeroed")
        table_split = sem("table_split")
        tparts_ready = sem("tparts_ready")
        mid_split = sem("mid_split")
        mparts_ready = sem("mparts_ready")
        onehot_ready = sem("onehot_ready")
        mid_onehot_ready = sem("mid_onehot_ready")
        looked_up = sem("looked_up")
        picked_ready = sem("picked_ready")
        mid_looked_up = sem("mid_looked_up")
        mid_ready = sem("mid_ready")
        idx_ready = sem("idx_ready")
        rows_in = [sem(f"rows_in{t}") for t in range(TILES)]
        rows_summed = [sem(f"rows_summed{t}") for t in range(TILES)]
        row_split = sem("row_split")
        rparts_ready = sem("rparts_ready")
        early_acc = sem("early_acc")
        early_ready = sem("early_ready")
        late_acc = sem("late_acc")
        late_ready = sem("late_ready")
        selected = sem("selected")
        factor_ready = sem("factor_ready")
        z_product = sem("z_product")
        dense_placed = sem("dense_placed")
        z_hi_ready = sem("z_hi_ready")
        z_lo_ready = sem("z_lo_ready")
        h1_acc = sem("h1_acc")
        h1_ready = sem("h1_ready")
        h2_acc = sem("h2_acc")
        h2_ready = sem("h2_ready")
        y_acc = sem("y_acc")
        y_ready = sem("y_ready")
        y_out = sem("y_out")

        block = ctx.enter_context(nc.Block())

        @block.sync
        def _(sp):
            sp.dma_start(idr[:, :], ids_rows).then_inc(ids_in, 16)
            sp.dma_start(fc[:, :], fconst).then_inc(consts_in, 16)

            def to_stage(use, n, src):
                if use >= STAGES:
                    sp.wait_ge(stage_summed, use - STAGES + 1)
                for a, b in ((0, SPLIT), (SPLIT, SHELVES)):
                    sp.dma_start(stage[a:b, use % STAGES, 0:n], src[a:b, :]).then_inc(stage_in[use % STAGES], 16)

            def load_group(g):
                n = PER_GROUP * GROUP_W[g] * DIM
                to_stage(g, n, tab8[:, g * n:(g + 1) * n] if g < G8 else tab10[:, (g - G8) * n:(g - G8 + 1) * n])

            def load_shelves(c, first, last):
                for g in range(first, last):
                    a, b = g * PER_GROUP, min((g + 1) * PER_GROUP, NHOT)
                    sp.dma_start(shelf_b[:, a:b, :],
                                 shelf_dram[bass.ds(c, 1), a:b, :].rearrange("c f n -> c (f n)").partition_broadcast(P)
                                 ).then_inc(shelf_in[g], 16)

            def load_slots(c):
                for lane in range(PER_GROUP):
                    sp.dma_start(slot_b[lane * LANE:(lane + 1) * LANE, :, :],
                                 slot_dram[bass.ds(c, 1), 0:NE, :].rearrange("c (g l) n -> l c g n", l=PER_GROUP)[lane]
                                 .partition_broadcast(LANE)).then_inc(slot_in[lane], 16)

            load_group(0)
            load_group(1)
            sp.wait_ge(slot_ready, 1)
            sp.dma_start(slot_dram.rearrange("c f n -> (c f) n"), slot_h[:, :]).then_inc(scratch_slot, 16)
            load_group(2)
            sp.dma_start(bc[:, 0:O_ID], bconst[:, 0:O_ID]).then_inc(select_in, 16)
            sp.dma_start(shelf_dram.rearrange("c f n -> (c f) n"), shelf_h[:, :]).then_inc(scratch_shelf, 16)
            sp.wait_ge(scratch_slot, 16)
            load_slots(0)
            for g in range(3, GROUPS):
                load_group(g)
            a = 0
            for k in range(KCH):
                for r0, r1 in ((0, SPLIT), (SPLIT, KROWS[k])):
                    sp.dma_start(w1_raw[r0:r1, k, :], w1[a + r0:a + r1, :]).then_inc(w1_in, 16)
                a += KROWS[k]
            sp.dma_start(w2_sb[:, :, :], w2.rearrange("(k p) n -> p k n", p=P)).then_inc(w2_in, 16)
            sp.wait_ge(scratch_shelf, 16)
            sp.wait_ge(onehot_ready, GROUPS)
            load_shelves(1, 0, 3)
            sp.wait_ge(picked_ready, GROUPS)
            load_slots(1)
            sp.wait_ge(rows_in[TILES - 1], 16 * NL)
            load_shelves(1, 3, GROUPS + 1)
            for i in range(NMID):
                for q in range(PIECES):
                    src = late_tables[NFETCH + i].rearrange("(q r) d -> q (r d)", q=SHELVES)
                    to_stage(GROUPS + i * PIECES + q, PIECE * DIM, src[:, q * PIECE * DIM:(q + 1) * PIECE * DIM])
            with sp.Fori(2, CHUNKS) as c:
                sp.wait_ge(onehot_ready, c * GROUPS)
                load_shelves(c, 0, GROUPS)
                sp.wait_ge(mid_onehot_ready, c - 1)
                load_shelves(c, GROUPS, GROUPS + 1)
                sp.wait_ge(picked_ready, c * GROUPS)
                load_slots(c)

        @block.gpsimd
        def _(pool):
            pool.dma_start(idc[:, :], ids_cols).then_inc(idc_in, 16)
            pool.wait_ge(idc_in, 16)

            def fetch(c, t, fields):
                pool.tensor_copy(idx[:, t, 0:fields], idc[:, bass.ds((c * TILES + t) * NL, fields)]
                                 ).then_inc(idx_ready, 1)
                pool.wait_ge(idx_ready, c * TILES + t + 1)
                pool.nop(nofuse=True)
                for k in range(fields):
                    pool.indirect_dma_start(rows[:, t, k, :], None, late_tables[k],
                                            bass.IndirectOffsetOnAxis(ap=idx[:, t, k:k + 1], axis=0)
                                            ).then_inc(rows_in[t], 16)

            for t in range(TILES):
                fetch(0, t, NL)
            with pool.Fori(1, CHUNKS) as c:
                for t in range(TILES):
                    pool.wait_ge(rows_summed[t], c)
                    fetch(c, t, NFETCH)

        def rows_landed(c, first):
            return 16 * NL if first else 16 * NL + 16 * NFETCH * c

        @block.vector
        def _(dve):
            dve.wait_ge(ids_in, 16)
            dve.wait_ge(consts_in, 16)
            dve.tensor_scalar(shelf_f[:, :], idr[:, :], fc[0:QR_ROWS, C_INV:C_INV + 1],
                              fc[0:QR_ROWS, C_OFF:C_OFF + 1], ALU.mult, ALU.add).then_inc(shelf_calc, 1)
            dve.wait_ge(shelf_calc, 1)
            dve.tensor_scalar(shelf_h[:, :], shelf_f[:, :], ROUND, ROUND, ALU.add,
                              ALU.subtract).then_inc(shelf_ready, 1)
            dve.wait_ge(shelf_ready, 1)
            dve.scalar_tensor_tensor(out=slot_h[:, :], in0=shelf_h[:, :], scalar=fc[0:QR_ROWS, C_NEGW:C_NEGW + 1],
                                     in1=idr[:, :], op0=ALU.mult, op1=ALU.add).then_inc(slot_ready, 1)
            dve.memset(tparts[:, :, :], 0.0).then_inc(zeroed, 1)
            dve.wait_ge(idc_in, 16)
            mid_ids = idc[:, :].rearrange("p (t k) -> p t k", k=NL)[:, :, NFETCH:NL]
            dve.tensor_scalar(mid_shelf[:, :, :], mid_ids, 1.0 / WMID, 0.5 / WMID - 0.5, ALU.mult,
                              ALU.add).then_inc(mid_calc, 1)
            dve.wait_ge(mid_calc, 1)
            dve.tensor_scalar(mid_shelf[:, :, :], mid_shelf[:, :, :], ROUND, ROUND, ALU.add,
                              ALU.subtract).then_inc(mid_calc, 1)
            dve.wait_ge(mid_calc, 2)
            dve.scalar_tensor_tensor(out=mid_slot[:, :].rearrange("p (t k) -> p t k", k=NMID),
                                     in0=mid_shelf[:, :, :], scalar=-float(WMID), in1=mid_ids, op0=ALU.mult,
                                     op1=ALU.add).then_inc(mid_calc, 1)

            def split(value, rest, part, calc, base, done):
                dve.tensor_copy(part(0), value).then_inc(calc, 1)
                dve.wait_ge(calc, base + 1)
                dve.tensor_tensor(rest(0), value, part(0), ALU.subtract).then_inc(calc, 1)
                dve.wait_ge(calc, base + 2)
                dve.tensor_copy(part(1), rest(0)).then_inc(calc, 1)
                dve.wait_ge(calc, base + 3)
                dve.tensor_tensor(rest(1), rest(0), part(1), ALU.subtract).then_inc(calc, 1)
                dve.wait_ge(calc, base + 4)
                dve.tensor_copy(part(2), rest(1)).then_inc(done, 1)

            def sum_stage(use, n, o):
                dve.wait_ge(stage_in[use % STAGES], 32 * (use // STAGES + 1))
                dve.tensor_reduce(o, stage[0:SHELVES, use % STAGES, 0:n * DIM].rearrange("p (r d) -> p r d", d=DIM),
                                  AX.X, ALU.add).then_inc(stage_summed, 1)

            def onehots(c, g):
                a, b = g * PER_GROUP, min((g + 1) * PER_GROUP, NHOT)
                if c is FIRST:
                    dve.wait_ge(shelf_copied, b)
                else:
                    dve.wait_ge(shelf_in[g], 16 * c)
                dve.tensor_scalar(onehot[0:SHELVES, a:b, :], shelf_b[0:SHELVES, a:b, :],
                                  fc[0:SHELVES, C_PART:C_PART + 1], None, ALU.is_equal
                                  ).then_inc(onehot_ready if g < GROUPS else mid_onehot_ready, 1)

            def pick(c, g, bank):
                if g == 0:
                    for lane in range(PER_GROUP):
                        dve.wait_ge(slot_in[lane], 16 * (c + 1))
                dve.wait_ge(looked_up, c * GROUPS + g + 1)
                j = C_J8 if GROUP_W[g] == W8 else C_J10
                dve.scalar_tensor_tensor(out=picked[:, g, :], in0=slot_b[:, g, :], scalar=fc[:, j:j + 1],
                                         in1=bank[:, :], op0=ALU.is_equal, op1=ALU.mult).then_inc(picked_ready, 1)

            def pick_middle(c, r):
                dve.wait_ge(mid_looked_up, (c - 1) * (TILES // MID_TILES) + r + 1)
                if r == 0:
                    dve.wait_ge(mid_calc, 3)
                else:
                    dve.wait_ge(mid_ready, ((c - 1) * TILES + r * MID_TILES) * NMID)
                for n in range(MID_TILES):
                    t = r * MID_TILES + n
                    for i in range(NMID):
                        at = n * NMID + i
                        dve.scalar_tensor_tensor(out=mid_picked[:, at, :], in0=slots,
                                                 scalar=mid_slot[:, bass.ds((c * TILES + t) * NMID + i, 1)],
                                                 in1=look[:, at * WMID:(at + 1) * WMID], op0=ALU.is_equal,
                                                 op1=ALU.mult, accum_out=rsum[:, t, NFETCH + i:NFETCH + i + 1]
                                                 ).then_inc(mid_ready, 1)

            def sum_rows(c, t, first):
                n = NL if first else NFETCH
                dve.wait_ge(rows_in[t], rows_landed(c, first))
                dve.tensor_reduce(rsum[:, t, 0:n], rows[:, t, 0:n, :], AX.X, ALU.add).then_inc(rows_summed[t], 1)

            def split_rows(c, first):
                for t in range(TILES):
                    dve.wait_ge(rows_summed[t], c + 1)
                if not first:
                    dve.wait_ge(mid_ready, c * TILES * NMID)
                split(rsum[:, :, :], lambda i: rrest[:, i, :, :], lambda i: rparts[:, :, i, :], row_split, 4 * c,
                      rparts_ready)

            def multiply(c, k):
                if not (k == 0 and c is FIRST):
                    dve.wait_ge(z_lo_ready, c * KCH + k)
                dve.wait_ge(factor_ready, c * KCH + k + 1)
                dve.tensor_tensor(z[0:KROWS[k], :], factor[0:KROWS[k], :], pb[0:KROWS[k], :],
                                  ALU.mult).then_inc(z_product, 1)

            def remainder(c, k):
                dve.wait_ge(z_hi_ready, c * KCH + k + 1)
                dve.tensor_tensor(z_lo[0:KROWS[k], k % ZRING, :], z[0:KROWS[k], :],
                                  z_hi[0:KROWS[k], k % ZRING, :].bitcast(F32), ALU.subtract).then_inc(z_lo_ready, 1)

            def sum_group(g):
                w = GROUP_W[g]
                sum_stage(g, PER_GROUP * w, tsum[0:SHELVES, g * PER_GROUP:(g + 1) * PER_GROUP, 0:w])

            def split_groups(n):
                a, b = BATCHES[n]
                w = GROUP_W[a]
                dve.wait_ge(stage_summed, b)
                if n == 0:
                    dve.wait_ge(zeroed, 1)
                fa, fb = a * PER_GROUP, b * PER_GROUP
                split(tsum[0:SHELVES, fa:fb, 0:w], lambda i: (trest, tsum)[i][0:SHELVES, fa:fb, 0:w],
                      lambda i: tparts[0:SHELVES, fa:fb, i * w:(i + 1) * w], table_split, 4 * n, tparts_ready)

            for g in (0, 1, 2):
                sum_group(g)
                onehots(FIRST, g)
            split_groups(0)
            for g in (3, 4):
                onehots(FIRST, g)
            for g in (0, 1):
                pick(0, g, FIRST_BANKS[g % 2])
            sum_group(3)
            pick(0, 2, FIRST_BANKS[0])
            onehots(FIRST, 5)
            sum_group(4)
            split_groups(1)
            onehots(FIRST, 6)
            sum_group(5)
            for g in (3, 4):
                pick(0, g, FIRST_BANKS[g % 2])
            sum_group(6)
            split_groups(2)
            for g in (5, 6):
                pick(0, g, FIRST_BANKS[g % 2])

            def split_w1(k):
                dve.wait_ge(w1_rounded, k + 1)
                dve.tensor_tensor(w1_lo[0:KROWS[k], k, :], w1_raw[0:KROWS[k], k, :],
                                  w1_hi[0:KROWS[k], k, :].bitcast(F32), ALU.subtract).then_inc(w1_split, 1)

            split_w1(0)
            sum_rows(0, 0, True)
            multiply(FIRST, 0)
            split_w1(1)
            remainder(0, 0)
            sum_rows(0, 1, True)
            multiply(0, 1)
            split_w1(2)
            remainder(0, 1)

            def sum_middle(n):
                i, q = divmod(n, PIECES)
                sum_stage(GROUPS + n, PIECE, msum[0:SHELVES, i, q * PIECE:(q + 1) * PIECE])
                if q == PIECES - 1:
                    dve.wait_ge(stage_summed, GROUPS + n + 1)
                    split(msum[0:SHELVES, i, :], lambda n: (mrest, msum)[n][0:SHELVES, i, :],
                          lambda n: mparts[0:SHELVES, i, n, :], mid_split, 4 * i, mparts_ready)

            def step(c, first=False, last=False):
                if not first and not last:
                    for g in range(AHEAD):
                        onehots(c + 1, g)
                for k in range(KCH):
                    if first and k >= 1 and k + 2 < KCH:
                        split_w1(k + 2)
                    for m in range(M1):
                        at = k * M1 + m
                        if not last:
                            if at == 4 and first:
                                onehots(c + 1, 0)
                            if at in GROUP_STEPS:
                                g = GROUP_STEPS.index(at)
                                if g + 1 < GROUPS and first:
                                    onehots(c + 1, g + 1)
                                pick(c + 1, g, look)
                            for g in HOT_STEPS:
                                if at == HOT_STEPS[g] and not first:
                                    onehots(c + 1, g)
                            if at == 22:
                                onehots(c + 1, GROUPS)
                        if m == {1: 1}.get(k, 1) and 0 < k < KCH - 1:
                            remainder(c, k + 1)
                        for t in ROW_STEPS:
                            if at == ROW_STEPS[t]:
                                sum_rows(c, t, first)
                        for t in NEXT_ROW_STEPS:
                            if at == NEXT_ROW_STEPS[t] and not last:
                                sum_rows(c + 1, t, False)
                        if at in MID_STEPS and not first:
                            pick_middle(c, MID_STEPS.index(at))
                        if at == 3:
                            split_rows(c, first)
                        if first and at in PIECE_STEPS:
                            sum_middle(PIECE_STEPS.index(at))
                    if k < 4:
                        multiply(c, k + 2)
                if not last:
                    pieces = list(range(len(PIECE_STEPS), NMID * PIECES)) if first else []
                    multiply(c + 1, 0)
                    for n in pieces[0:1]:
                        sum_middle(n)
                    remainder(c + 1, 0)
                    multiply(c + 1, 1)
                    for n in pieces[1:2]:
                        sum_middle(n)
                    remainder(c + 1, 1)
                    for n in pieces[2:]:
                        sum_middle(n)

            step(0, first=True)
            with dve.Fori(1, CHUNKS - 1) as c:
                step(c)
            step(CHUNKS - 1, last=True)

        @block.scalar
        def _(act):
            act.dma_start(bc[:, O_ID:], bconst[:, O_ID:]).then_inc(bconst_in, 16)
            act.dma_start(dense[:, :], dense_t[:, 0:CHUNK]).then_inc(dense_in, 16)
            act.dma_start(cols[:, :], columns).then_inc(w2_in, 16)
            for f in range(NE):
                act.wait_ge(shelf_spread, f + 1)
                act.copy(shelf_b[:, f, :], SPREAD_BANKS[f % 3][:, :]).then_inc(shelf_copied, 1)
            act.wait_ge(w1_in, 16 * 2 * KCH)
            for k in range(KCH):
                act.copy(w1_hi[0:KROWS[k], k, :], w1_raw[0:KROWS[k], k, :]).then_inc(w1_rounded, 1)

            def round_z(c, k, last=False):
                act.wait_ge(selected, c * KCH + k + 1)
                act.copy(factor[0:KROWS[k], :], pa[0:KROWS[k], :]).then_inc(factor_ready, 1)
                act.wait_ge(z_product, c * KCH + k + 1)
                if k == KCH - 1:
                    act.wait_ge(dense_in, 16 * (c + 1))
                    act.copy(z[0:DENSE, :], dense[:, :]).then_inc(dense_placed, 1)
                    act.wait_ge(dense_placed, c + 1)
                    if not last:
                        act.dma_start(dense[:, :], dense_t[:, bass.ds((c + 1) * CHUNK, CHUNK)]).then_inc(dense_in, 16)
                act.copy(z_hi[0:KROWS[k], k % ZRING, :], z[0:KROWS[k], :]).then_inc(z_hi_ready, 1)

            act.wait_ge(early_acc, 1)
            act.copy(s_early[:, :], early[0:RE, :]).then_inc(early_ready, 1)
            act.wait_ge(w2_in, 32)
            round_z(0, 0)
            round_z(0, 1)

            def step(c, first=False, last=False):
                for k in range(KCH):
                    if k == 1:
                        act.wait_ge(late_acc, c + 1)
                        act.copy(s_late[:, :], look[0:RL, :]).then_inc(late_ready, 1)
                    if k < 4:
                        round_z(c, k + 2, last)
                for m in range(M1):
                    if m == M2 and not last:
                        act.wait_ge(early_acc, c + 2)
                        act.copy(s_early[:, :], early[0:RE, :]).then_inc(early_ready, 1)
                    act.wait_ge(h1_acc, c * M1 + m + 1)
                    act.activation(h1[:, m, :], ph[m][:, :], ACT.Relu, bias=b1_sb[:, m:m + 1]).then_inc(h1_ready, 1)
                if not last:
                    round_z(c + 1, 0)
                    round_z(c + 1, 1)
                for m in range(M2):
                    act.wait_ge(h2_acc, c * M2 + m + 1)
                    act.activation(h2[:, m, :], ph[m][:, :], ACT.Relu, bias=b2_sb[:, m:m + 1]).then_inc(h2_ready, 1)
                act.wait_ge(y_acc, c + 1)
                if not first:
                    act.wait_ge(y_out, 16 * c)
                act.copy(y_sb[:, :], ph[2][0:1, :]).then_inc(y_ready, 1)
                act.wait_ge(y_ready, c + 1)
                act.dma_start(out[:, bass.ds(c * CHUNK, CHUNK)], y_sb[:, :]).then_inc(y_out, 16)

            step(0, first=True)
            with act.Fori(1, CHUNKS - 1) as c:
                step(c)
            step(CHUNKS - 1, last=True)
            act.wait_ge(y_out, 16 * CHUNKS)

        @block.tensor
        def _(pe):
            pe.wait_ge(bconst_in, 16)

            def lookup(c, g, bank):
                pe.wait_ge(onehot_ready, c * GROUPS + g + 1)
                for lane in range(PER_GROUP):
                    f = g * PER_GROUP + lane
                    mm = pe.matmul(bank[lane * LANE:(lane + 1) * LANE, :], tparts[0:SHELVES, f, :],
                                   onehot[0:SHELVES, f, :], start=True, stop=True)
                mm.then_inc(looked_up, 1)

            def sum_lanes(c, g):
                pe.wait_ge(picked_ready, c * GROUPS + g + 1)
                mm = pe.matmul(early[0:RE, :], sum_w[:, g, :], picked[:, g, :], start=(g == 0),
                               stop=(g == GROUPS - 1))
                if g == GROUPS - 1:
                    mm.then_inc(early_acc, 1)

            def lookup_middle(c, r):
                if r == 0:
                    pe.wait_ge(mid_onehot_ready, c)
                    pe.wait_ge(mparts_ready, NMID)
                else:
                    pe.wait_ge(mid_ready, ((c - 1) * TILES + r * MID_TILES) * NMID)
                for n in range(MID_TILES):
                    t = r * MID_TILES + n
                    for i in range(NMID):
                        a = (n * NMID + i) * WMID
                        for part in range(PARTS):
                            mm = pe.matmul(look[:, a:a + WMID], onehot[0:SHELVES, NE + i, t * P:(t + 1) * P],
                                           mparts[0:SHELVES, i, part, :], start=(part == 0), stop=(part == PARTS - 1))
                mm.then_inc(mid_looked_up, 1)

            def transpose_late(c, first):
                pe.wait_ge(rparts_ready, c + 1)
                if not first:
                    pe.wait_ge(mid_ready, c * TILES * NMID)
                for t in range(TILES):
                    mm = pe.matmul(look[0:RL, t * P:(t + 1) * P], rparts[:, t, :, :].rearrange("p a f -> p (a f)"),
                                   ident, start=True, stop=True)
                mm.then_inc(late_acc, 1)

            def select(c, k):
                n = KROWS[k]

                def pick_rows(bank, o_early=None, o_late=None):
                    if o_early is not None:
                        mm = pe.matmul(bank[0:n, :], bc[0:RE, o_early:o_early + n], s_early[:, :],
                                       start=True, stop=o_late is None)
                    if o_late is not None:
                        mm = pe.matmul(bank[0:n, :], bc[0:RL, o_late:o_late + n], s_late[:, :],
                                       start=o_early is None, stop=True)
                    return mm

                if k == 0:
                    pe.wait_ge(early_ready, c + 1)
                if k == 3:
                    pe.wait_ge(late_ready, c + 1)
                if not (k == 0 and c is FIRST):
                    pe.wait_ge(z_product, c * KCH + k)
                pick_rows(pa, O_E1 + k * P, O_L1 if k == 5 else None)
                if k < 3:
                    pick_rows(pb, O_E2 + k * P).then_inc(selected, 1)
                else:
                    pick_rows(pb, None, O_L2 + (k - 3) * P).then_inc(selected, 1)

            pe.wait_ge(shelf_ready, 1)
            for f in range(NE):
                if f >= 3:
                    pe.wait_ge(shelf_copied, f - 2)
                pe.matmul(SPREAD_BANKS[f % 3][:, :], ident[0:QR_ROWS, f:f + 1].to_broadcast([QR_ROWS, P]),
                          shelf_h[:, :], start=True, stop=True).then_inc(shelf_spread, 1)
            pe.wait_ge(select_in, 16)
            for a, b in BATCHES:
                for g in range(a, b):
                    pe.wait_ge(tparts_ready, BATCHES.index((a, b)) + 1)
                    if g >= 2:
                        pe.wait_ge(picked_ready, g - 1)
                    lookup(0, g, FIRST_BANKS[g % 2])
                    if g > 0:
                        sum_lanes(0, g - 1)
            sum_lanes(0, GROUPS - 1)
            select(FIRST, 0)
            select(0, 1)
            pe.wait_ge(w2_in, 32)

            def step(c, first=False, last=False):
                for k in range(KCH):
                    pe.wait_ge(z_hi_ready, c * KCH + k + 1)
                    if first:
                        pe.wait_ge(w1_split, k + 1)
                    n = KROWS[k]
                    for m in range(M1):
                        if k == 0 and m == 2 and not first:
                            pe.wait_ge(y_ready, c)
                        hi, lo = w1_hi[0:n, k, m * P:(m + 1) * P], w1_lo[0:n, k, m * P:(m + 1) * P]
                        pe.matmul(ph[m][:, :], hi, z_hi[0:n, k % ZRING, :], start=(k == 0), stop=False)
                        pe.matmul(ph[m][:, :], lo, z_hi[0:n, k % ZRING, :], start=False, stop=False)
                        if m == 0:
                            pe.wait_ge(z_lo_ready, c * KCH + k + 1)
                        mm = pe.matmul(ph[m][:, :], hi, z_lo[0:n, k % ZRING, :], start=False, stop=(k == KCH - 1))
                        if k == KCH - 1:
                            mm.then_inc(h1_acc, 1)
                        at = k * M1 + m
                        if not last and at in GROUP_STEPS:
                            g = GROUP_STEPS.index(at)
                            if g > 0:
                                pe.wait_ge(picked_ready, (c + 1) * GROUPS + g)
                            else:
                                pe.wait_ge(late_ready, c + 1)
                            lookup(c + 1, g, look)
                        if not last and at in SUM_STEPS:
                            sum_lanes(c + 1, SUM_STEPS.index(at))
                        if not first and at in MID_STEPS:
                            lookup_middle(c, MID_STEPS.index(at))
                        if at == 5:
                            transpose_late(c, first)
                    if k < 4:
                        select(c, k + 2)
                if not last:
                    select(c + 1, 0)
                for k in range(M1):
                    pe.wait_ge(h1_ready, c * M1 + max(k + 1, M2))
                    for m in range(M2):
                        mm = pe.matmul(ph[m][:, :], w2_sb[:, k, m * P:(m + 1) * P], h1[:, k, :],
                                       start=(k == 0), stop=(k == M1 - 1))
                        if k == M1 - 1:
                            mm.then_inc(h2_acc, 1)
                    if k == 1 and not last:
                        select(c + 1, 1)
                for m in range(M2):
                    pe.wait_ge(h2_ready, c * M2 + m + 1)
                    mm = pe.matmul(ph[2][0:1, :], w3_sb[:, m:m + 1], h2[:, m, :], start=(m == 0),
                                   stop=(m == M2 - 1))
                mm.then_inc(y_acc, 1)

            step(0, first=True)
            with pe.Fori(1, CHUNKS - 1) as c:
                step(c)
            step(CHUNKS - 1, last=True)


def _pairs():
    early = [(a, b) for a in range(NE) for b in range(a + 1, NE)]
    late = [(a, b) for a in range(NE) for b in range(NE, FIELDS)]
    late += [(a, b) for a in range(NE, FIELDS) for b in range(a + 1, FIELDS)]
    late[2 * P:2 * P] = [None] * DENSE
    return [early[0:P], early[P:2 * P], early[2 * P:], late[0:P], late[P:2 * P], late[2 * P:]]


def _w1_rows(np):
    index = {pair: n for n, pair in enumerate(zip(*(x.tolist() for x in np.triu_indices(FIELDS, k=1))))}
    rows, dense = [], PAIRS
    for chunk in _pairs():
        for pair in chunk:
            if pair is None:
                rows.append(dense)
                dense += 1
            else:
                rows.append(index[tuple(sorted((ORDER[pair[0]], ORDER[pair[1]])))])
    return np.array(rows)


def _shape_constants(np):
    fconst = np.zeros((P, 6), np.float32)
    p = np.arange(P)
    fconst[:, C_PART] = p
    for col, w in ((C_J8, W8), (C_J10, W10)):
        r = p % LANE
        fconst[:, col] = np.where(r < PARTS * w, r % w, -1)
    for row in range(QR_ROWS):
        f = row % NHOT
        w = VOCAB[ORDER[f]] // SHELVES if f < NE else WMID
        fconst[row, C_INV] = 1.0 / w
        fconst[row, C_OFF] = 0.5 / w - 0.5
        fconst[row, C_NEGW] = -w
    bconst = np.zeros((P, NCONST), np.float32)
    for g in range(GROUPS):
        w = GROUP_W[g]
        for lane in range(PER_GROUP):
            for i in range(PARTS):
                a = lane * LANE + i * w
                bconst[a:a + w, O_SUM + g * RE + i * NE + g * PER_GROUP + lane] = 1
    for k, chunk in enumerate(_pairs()):
        for r, pair in enumerate(chunk):
            for place, o_early, o_late in zip(pair or (), (O_E1 + k * P, O_E2 + k * P), (O_L1, O_L2 + (k - 3) * P)):
                for i in range(PARTS):
                    if place < NE:
                        bconst[i * NE + place, o_early + r] = 1
                    else:
                        bconst[i * NL + place - NE, o_late + r] = 1
    bconst[p, O_ID + p] = 1
    bconst[:, O_SLOT:] = np.arange(WMID)
    return fconst, bconst


def kernel(**inputs):
    import numpy as np
    import concourse.bacc as bacc
    from concourse.bass_utils import run_bass_kernel_spmd

    nc = bacc.Bacc("TRN2", target_bir_lowering=False, num_devices=1)
    arrays = {}

    def dram(name, a):
        a = np.ascontiguousarray(a)
        arrays[name] = a
        return nc.dram_tensor(name, a.shape, mybir.dt.from_np(a.dtype), kind="ExternalInput").ap()

    ids = np.asarray(inputs["ids"])
    hot = np.array(EARLY + LATE[NFETCH:])
    by_field = ids.T[hot].reshape(NHOT, CHUNKS, CHUNK).transpose(1, 0, 2).reshape(QR_ROWS, CHUNK)
    by_row = ids[:, np.array(LATE)].reshape(BATCH // P, P, NL).transpose(1, 0, 2).reshape(P, -1)

    def shelves(fields):
        return np.concatenate([np.asarray(inputs[f"tbl_{f}"]).reshape(SHELVES, -1) for f in fields], axis=1)

    columns = np.concatenate([np.asarray(inputs[n]).reshape(-1, P).T for n in ("W_top3", "b_top1", "b_top2")], axis=1)
    fconst, bconst = _shape_constants(np)
    out = nc.dram_tensor("out", (1, BATCH), F32, kind="ExternalOutput").ap()
    build_tower(
        nc, dram("ids_rows", by_field), dram("ids_cols", by_row), dram("dense_t", np.asarray(inputs["dense_ctx"]).T),
        dram("tab8", shelves(F8)), dram("tab10", shelves(F10)), [dram(f"tab_{f}", inputs[f"tbl_{f}"]) for f in LATE],
        dram("w1", np.asarray(inputs["W_top1"])[_w1_rows(np)]), dram("w2", inputs["W_top2"]),
        dram("columns", columns), dram("fconst", fconst), dram("bconst", bconst.astype(np.dtype("bfloat16"))), out)
    r = run_bass_kernel_spmd(nc, [arrays], core_ids=[0])
    return r.results[0]["out"].reshape(BATCH, 1)
```

```python
from contextlib import ExitStack

import concourse.bass as bass
from concourse import mybir

ALU = mybir.AluOpType
ACT = mybir.ActivationFunctionType
AX = mybir.AxisListType
F32 = mybir.dt.float32
BF16 = mybir.dt.bfloat16
F32R = mybir.dt.float32r
I32 = mybir.dt.int32

FIRST = 0
P = 128
BATCH = 2048
CHUNK = 512
CHUNKS = BATCH // CHUNK
TILES = CHUNK // P
DIM = 64
FIELDS = 39
DENSE = 16
APPENDED = DENSE + 1

VOCAB = [125000, 1000, 1250, 1000, 125000, 125000, 1250, 12500, 12500, 12500, 1000, 1250, 1000, 12500, 12500,
         1250, 1000, 12500, 1250, 1000, 1000, 1000, 1250, 1000, 1000, 12500, 1250, 1000, 1000, 1000, 1000,
         1000, 1000, 1000, 1250, 12500, 1000, 1000, 1000]

SHELVES = 125
SPLIT = 112
W8, W10, WMID = 8, 10, 100
F8 = [f for f in range(FIELDS) if VOCAB[f] == SHELVES * W8]
F10 = [f for f in range(FIELDS) if VOCAB[f] == SHELVES * W10]
EARLY = F8 + F10
LARGE = [f for f in range(FIELDS) if VOCAB[f] > SHELVES * WMID]
MIDDLE = [f for f in range(FIELDS) if VOCAB[f] == SHELVES * WMID]
NMID = 2
LATE = LARGE + MIDDLE
ORDER = EARLY + LATE
NE, NL = len(EARLY), len(LATE)
NFETCH = NL - NMID
NHOT = NE + NMID

LANE = 32
PER_GROUP = P // LANE
GROUPS = NE // PER_GROUP
GROUP_W = [W8 if ORDER[g * PER_GROUP] in F8 else W10 for g in range(GROUPS)]
G8 = GROUP_W.count(W8)
BATCHES = [(0, 3), (3, G8), (G8, GROUPS)]
PARTS = 3
RE, RL = PARTS * NE, PARTS * NL
PIECE = 25
PIECES = WMID // PIECE
STAGES = 4
W_USES = (GROUPS, GROUPS + 1)
PIECE_USE = GROUPS + 2

PAIRS = FIELDS * (FIELDS - 1) // 2
EARLY_PAIRS = NE * (NE - 1) // 2
KCH = 6
KROWS = [P, P, EARLY_PAIRS - 2 * P, P, P, PAIRS - EARLY_PAIRS + APPENDED - 2 * P]
H1, H2 = 512, 256
M1, M2 = H1 // P, H2 // P
ROUND = 12582912.0
QR_ROWS = CHUNKS * NHOT

C_PART, C_J8, C_J10, C_INV, C_OFF, C_NEGW = range(6)
O_SUM = 0
O_E1 = O_SUM + GROUPS * RE
O_E2 = O_E1 + KCH * P
O_L1 = O_E2 + 3 * P
O_L2 = O_L1 + P
O_ID = O_L2 + 3 * P
O_SLOT = O_ID + P
NCONST = O_SLOT + WMID

MID_TILES = min(TILES, CHUNK // (NMID * WMID))
MID_STEPS = [2 * r for r in range(TILES // MID_TILES)]
LATE_STEP = 5
GROUP_STEPS = [7, 9, 11, 13, 15, 17, 19]
SUM_STEPS = GROUP_STEPS[1:] + [21]
HOT_START = 1
HOT_STEPS = {1: 4, 2: 8, 3: 10, 4: 12, 5: 14, 6: 16}
HOT_STEPS_FIRST = {0: 4} | {g: GROUP_STEPS[g - 1] for g in range(1, GROUPS)}
MID_HOT_STEP = 22
ROW_STEPS = {2: 2, 3: 3}
NEXT_ROW_STEP = 15
PIECE_STEPS = [9, 12, 14, 16, 18, 20, 22]
ZRING = 3


def build_tower(nc, ids_rows, ids_cols, dense_t, tab8, tab10, late_tables, w1, w2, columns, fconst, bconst, out):
    assert EARLY_PAIRS <= 3 * P and sum(KROWS) == w1.shape[0] and QR_ROWS <= P
    with ExitStack() as ctx:
        def sb(name, shape, dt):
            return ctx.enter_context(nc.sbuf_tensor(name, shape, dt))

        def ps(name):
            return ctx.enter_context(nc.psum_tensor(name, [P, CHUNK], F32))

        def sem(name):
            return ctx.enter_context(nc.semaphore(name))

        shelf_dram = nc.dram_tensor("shelf_scratch", (CHUNKS, NHOT, CHUNK), BF16, kind="Internal").ap()
        slot_dram = nc.dram_tensor("slot_scratch", (CHUNKS, NHOT, CHUNK), BF16, kind="Internal").ap()

        fc = sb("fc", [P, 6], F32)
        bc = sb("bc", [P, NCONST], BF16)
        ids_h = sb("ids_h", [QR_ROWS, 2 * CHUNK], BF16)
        shelf_h, slot_h = ids_h[:, 0:CHUNK], ids_h[:, CHUNK:]
        y_sb = ids_h[0:1, :].bitcast(F32)
        idc = sb("idc", [P, (CHUNKS + 1) * TILES * NL], I32)
        idx = sb("idx", [P, TILES, NFETCH], I32)
        mid_shelf = sb("mid_shelf", [P, CHUNKS * TILES, NMID], F32)
        mid_slot = sb("mid_slot", [P, CHUNKS * TILES * NMID], F32)
        stage = sb("stage", [P, STAGES, PER_GROUP * W10 * DIM], F32)
        tsum = sb("tsum", [P, NE, W10], F32)
        trest = sb("trest", [P, NE, W10], F32)
        tparts = sb("tparts", [P, NE, LANE], BF16)
        mid_work = sb("mid_work", [P, 2 * NMID, WMID], F32)
        msum, mrest = mid_work[:, 0:NMID, :], mid_work[:, NMID:, :]
        mid_picked = mid_work
        mparts = sb("mparts", [P, NMID, PARTS, WMID], BF16)
        shelf_b = sb("shelf_b", [P, NHOT, CHUNK], BF16)
        slot_b = sb("slot_b", [P, GROUPS, CHUNK], BF16)
        onehot = sb("onehot", [P, NHOT, CHUNK], BF16)
        picked = sb("picked", [P, 2, CHUNK], BF16)
        assert MID_TILES <= 2
        rows = sb("rows", [P, TILES, NL, DIM], F32)
        rsum = sb("rsum", [P, TILES, NL], F32)
        rrest = sb("rrest", [P, 2, TILES, NL], F32)
        rparts = sb("rparts", [P, TILES, PARTS, NL], BF16)
        s_early = sb("s_early", [RE, CHUNK], BF16)
        s_late = sb("s_late", [RL, CHUNK], BF16)
        factor = sb("factor", [P, CHUNK], F32)
        z = sb("z", [P, CHUNK], F32)
        idr = factor[0:QR_ROWS, :].bitcast(I32)
        shelf_f = z[0:QR_ROWS, :]
        z_hi = sb("z_hi", [P, ZRING, CHUNK], F32R)
        z_lo = sb("z_lo", [P, ZRING, CHUNK], F32R)
        dense = sb("dense", [APPENDED, CHUNK], F32)
        w1_hi = sb("w1_hi", [P, KCH, H1], F32R)
        w1_lo = sb("w1_lo", [P, KCH, H1], F32R)
        w2_hi = sb("w2_hi", [P, M1, H2], F32R)
        w2_lo = sb("w2_lo", [P, M1, H2], F32R)
        raw_a, raw_b = stage[:, W_USES[0] % STAGES, :], stage[:, W_USES[1] % STAGES, :]
        w1_raw = [raw_a[:, k * H1:(k + 1) * H1] for k in range(KCH - 1)] + [raw_b[:, 0:H1]]
        w2_raw = raw_b[:, H1:H1 + M1 * H2].rearrange("p (k n) -> p k n", n=H2)
        cols = sb("cols", [P, 2 * M2], F32)
        w3_sb, b2_sb = cols[:, 0:M2], cols[:, M2:]
        h2 = sb("h2", [P, M2, CHUNK], F32)
        h1_hi = sb("h1_hi", [P, M1, CHUNK], F32R)
        h1_lo = sb("h1_lo", [P, M1, CHUNK], F32R)

        look = ps("look")
        early = ps("early")
        pa = ps("pa")
        pb = ps("pb")
        ph = [ps(f"ph{m}") for m in range(M1)]

        FIRST_BANKS = [look, ph[3]]
        SPREAD_BANKS = ph[0:3]
        sum_w = bc[:, O_SUM:O_E1].rearrange("p (g s) -> p g s", g=GROUPS)
        ident = bc[:, O_ID:O_ID + P]
        slots = bc[:, O_SLOT:NCONST]

        ids_in = sem("ids_in")
        consts_in = sem("consts_in")
        bconst_in = sem("bconst_in")
        select_in = sem("select_in")
        idc_in = sem("idc_in")
        dense_in = sem("dense_in")
        w1_in = [sem(f"w1_in{k}") for k in range(KCH)]
        w2_in = sem("w2_in")
        columns_in = sem("columns_in")
        w1_rounded = sem("w1_rounded")
        w1_split = sem("w1_split")
        w2_rounded = sem("w2_rounded")
        w2_split = sem("w2_split")
        stage_in = [sem(f"stage_in{i}") for i in range(STAGES)]
        stage_free = [sem(f"stage_free{i}") for i in range(STAGES)]
        shelf_calc = sem("shelf_calc")
        shelf_spread = sem("shelf_spread")
        shelf_copied = sem("shelf_copied")
        shelf_ready = sem("shelf_ready")
        slot_ready = sem("slot_ready")
        mid_calc = sem("mid_calc")
        scratch_shelf = sem("scratch_shelf")
        scratch_slot = sem("scratch_slot")
        shelf_in = [sem(f"shelf_in{g}") for g in range(GROUPS + 1)]
        slot_in = [sem(f"slot_in{n}") for n in range(PER_GROUP)]
        zeroed = sem("zeroed")
        table_split = sem("table_split")
        tparts_ready = sem("tparts_ready")
        mid_split = sem("mid_split")
        mparts_ready = sem("mparts_ready")
        onehot_ready = sem("onehot_ready")
        mid_onehot_ready = sem("mid_onehot_ready")
        looked_up = sem("looked_up")
        picked_ready = sem("picked_ready")
        mid_looked_up = sem("mid_looked_up")
        mid_ready = sem("mid_ready")
        idx_ready = [sem(f"idx_ready{t}") for t in range(TILES)]
        rows_in = [sem(f"rows_in{t}") for t in range(TILES)]
        rows_summed = [sem(f"rows_summed{t}") for t in range(TILES)]
        row_split = sem("row_split")
        rparts_ready = sem("rparts_ready")
        early_acc = sem("early_acc")
        early_ready = sem("early_ready")
        late_acc = sem("late_acc")
        late_ready = sem("late_ready")
        selected = sem("selected")
        factor_ready = sem("factor_ready")
        z_product = sem("z_product")
        dense_placed = sem("dense_placed")
        z_hi_ready = sem("z_hi_ready")
        z_lo_ready = sem("z_lo_ready")
        h1_acc = sem("h1_acc")
        h1_hi_ready = sem("h1_hi_ready")
        h1_lo_ready = sem("h1_lo_ready")
        h2_acc = sem("h2_acc")
        h2_ready = sem("h2_ready")
        y_acc = sem("y_acc")
        y_ready = sem("y_ready")
        y_out = sem("y_out")

        def earlier(use):
            return use // STAGES - sum(w < use and (use - w) % STAGES == 0 for w in W_USES)

        block = ctx.enter_context(nc.Block())

        @block.sync
        def _(sp):
            sp.dma_start(idr[:, :], ids_rows).then_inc(ids_in, 16)
            sp.dma_start(fc[:, :], fconst).then_inc(consts_in, 16)

            def to_stage(use, n, src):
                if use >= STAGES:
                    sp.wait_ge(stage_free[use % STAGES], earlier(use))
                for a, b in ((0, SPLIT), (SPLIT, SHELVES)):
                    sp.dma_start(stage[a:b, use % STAGES, 0:n], src[a:b, :]).then_inc(stage_in[use % STAGES], 16)

            def load_group(g):
                n = PER_GROUP * GROUP_W[g] * DIM
                to_stage(g, n, tab8[:, g * n:(g + 1) * n] if g < G8 else tab10[:, (g - G8) * n:(g - G8 + 1) * n])

            def load_shelves(c, first, last):
                for g in range(first, last):
                    a, b = g * PER_GROUP, min((g + 1) * PER_GROUP, NHOT)
                    sp.dma_start(shelf_b[:, a:b, :],
                                 shelf_dram[bass.ds(c, 1), a:b, :].rearrange("c f n -> c (f n)").partition_broadcast(P)
                                 ).then_inc(shelf_in[g], 16)

            def load_slots(c):
                for lane in range(PER_GROUP):
                    sp.dma_start(slot_b[lane * LANE:(lane + 1) * LANE, :, :],
                                 slot_dram[bass.ds(c, 1), 0:NE, :].rearrange("c (g l) n -> l c g n", l=PER_GROUP)[lane]
                                 .partition_broadcast(LANE)).then_inc(slot_in[lane], 16)

            load_group(0)
            load_group(1)
            sp.wait_ge(slot_ready, 1)
            sp.dma_start(slot_dram.rearrange("c f n -> (c f) n"), slot_h[:, :]).then_inc(scratch_slot, 16)
            load_group(2)
            sp.dma_start(bc[:, 0:O_ID], bconst[:, 0:O_ID]).then_inc(select_in, 16)
            sp.dma_start(shelf_dram.rearrange("c f n -> (c f) n"), shelf_h[:, :]).then_inc(scratch_shelf, 16)
            sp.wait_ge(scratch_slot, 16)
            load_slots(0)
            for g in range(3, GROUPS):
                load_group(g)
            for use in W_USES:
                sp.wait_ge(stage_free[use % STAGES], earlier(use))
            a = 0
            for k in range(KCH):
                for r0, r1 in ((0, SPLIT), (SPLIT, KROWS[k])):
                    sp.dma_start(w1_raw[k][r0:r1, :], w1[a + r0:a + r1, :]).then_inc(w1_in[k], 16)
                a += KROWS[k]
            sp.dma_start(w2_raw[:, :, :], w2.rearrange("(k p) n -> p k n", p=P)).then_inc(w2_in, 16)
            sp.wait_ge(scratch_shelf, 16)
            sp.wait_ge(onehot_ready, GROUPS)
            load_shelves(1, 0, 3)
            sp.wait_ge(picked_ready, GROUPS)
            load_slots(1)

            def load_pieces(first, end):
                for n in range(first, end):
                    if n == W_USES[0] + STAGES - PIECE_USE:
                        sp.wait_ge(w1_split, KCH)
                        sp.wait_ge(w2_split, 1)
                    i, q = divmod(n, PIECES)
                    src = late_tables[NFETCH + i].rearrange("(q r) d -> q (r d)", q=SHELVES)
                    to_stage(PIECE_USE + n, PIECE * DIM, src[:, q * PIECE * DIM:(q + 1) * PIECE * DIM])

            sp.wait_ge(rows_in[TILES - 1], 16 * NL)
            load_shelves(1, 3, GROUPS + 1)
            load_pieces(0, NMID * PIECES)
            with sp.Fori(2, CHUNKS) as c:
                sp.wait_ge(onehot_ready, c * GROUPS)
                load_shelves(c, 0, GROUPS)
                sp.wait_ge(mid_onehot_ready, c - 1)
                load_shelves(c, GROUPS, GROUPS + 1)
                sp.wait_ge(picked_ready, c * GROUPS)
                load_slots(c)

        @block.gpsimd
        def _(pool):
            pool.dma_start(idc[:, :], ids_cols).then_inc(idc_in, 16)
            pool.wait_ge(idc_in, 16)

            def fetch(t, fields, index):
                for k in range(fields):
                    pool.indirect_dma_start(rows[:, t, k, :], None, late_tables[k],
                                            bass.IndirectOffsetOnAxis(ap=index(k), axis=0)).then_inc(rows_in[t], 16)

            for t in range(TILES):
                fetch(t, NL, lambda k: idc[:, t * NL + k:t * NL + k + 1])
            with pool.Fori(1, CHUNKS) as c:
                for t in range(TILES):
                    pool.wait_ge(idx_ready[t], c)
                    pool.nop(nofuse=True)
                    fetch(t, NFETCH, lambda k: idx[:, t, k:k + 1])

        def rows_landed(c, first):
            return 16 * NL if first else 16 * NL + 16 * NFETCH * c

        @block.vector
        def _(dve):
            dve.wait_ge(ids_in, 16)
            dve.wait_ge(consts_in, 16)
            dve.tensor_scalar(shelf_f[:, :], idr[:, :], fc[0:QR_ROWS, C_INV:C_INV + 1],
                              fc[0:QR_ROWS, C_OFF:C_OFF + 1], ALU.mult, ALU.add).then_inc(shelf_calc, 1)
            dve.wait_ge(shelf_calc, 1)
            dve.tensor_scalar(shelf_h[:, :], shelf_f[:, :], ROUND, ROUND, ALU.add,
                              ALU.subtract).then_inc(shelf_ready, 1)
            dve.wait_ge(shelf_ready, 1)
            dve.scalar_tensor_tensor(out=slot_h[:, :], in0=shelf_h[:, :], scalar=fc[0:QR_ROWS, C_NEGW:C_NEGW + 1],
                                     in1=idr[:, :], op0=ALU.mult, op1=ALU.add).then_inc(slot_ready, 1)
            dve.memset(tparts[:, :, :], 0.0).then_inc(zeroed, 1)
            dve.wait_ge(idc_in, 16)
            mid_ids = idc[:, 0:CHUNKS * TILES * NL].rearrange("p (t k) -> p t k", k=NL)[:, :, NFETCH:NL]
            dve.tensor_scalar(mid_shelf[:, :, :], mid_ids, 1.0 / WMID, 0.5 / WMID - 0.5, ALU.mult,
                              ALU.add).then_inc(mid_calc, 1)
            dve.wait_ge(mid_calc, 1)
            dve.tensor_scalar(mid_shelf[:, :, :], mid_shelf[:, :, :], ROUND, ROUND, ALU.add,
                              ALU.subtract).then_inc(mid_calc, 1)
            dve.wait_ge(mid_calc, 2)
            dve.scalar_tensor_tensor(out=mid_slot[:, :].rearrange("p (t k) -> p t k", k=NMID),
                                     in0=mid_shelf[:, :, :], scalar=-float(WMID), in1=mid_ids, op0=ALU.mult,
                                     op1=ALU.add).then_inc(mid_calc, 1)

            def split(value, rest, part, calc, base, done):
                dve.tensor_copy(part(0), value).then_inc(calc, 1)
                dve.wait_ge(calc, base + 1)
                dve.tensor_tensor(rest(0), value, part(0), ALU.subtract).then_inc(calc, 1)
                dve.wait_ge(calc, base + 2)
                dve.tensor_copy(part(1), rest(0)).then_inc(calc, 1)
                dve.wait_ge(calc, base + 3)
                dve.tensor_tensor(rest(1), rest(0), part(1), ALU.subtract).then_inc(calc, 1)
                dve.wait_ge(calc, base + 4)
                dve.tensor_copy(part(2), rest(1)).then_inc(done, 1)

            def sum_stage(use, n, o):
                dve.wait_ge(stage_in[use % STAGES], 32 * (earlier(use) + 1))
                dve.tensor_reduce(o, stage[0:SHELVES, use % STAGES, 0:n * DIM].rearrange("p (r d) -> p r d", d=DIM),
                                  AX.X, ALU.add).then_inc(stage_free[use % STAGES], 1)

            def wait_summed(engine, first, end):
                for use in range(max(first, end - STAGES), end):
                    engine.wait_ge(stage_free[use % STAGES], earlier(use) + 1)

            def onehots(c, g):
                a, b = g * PER_GROUP, min((g + 1) * PER_GROUP, NHOT)
                if c is FIRST:
                    dve.wait_ge(shelf_copied, b)
                else:
                    dve.wait_ge(shelf_in[g], 16 * c)
                dve.tensor_scalar(onehot[0:SHELVES, a:b, :], shelf_b[0:SHELVES, a:b, :],
                                  fc[0:SHELVES, C_PART:C_PART + 1], None, ALU.is_equal
                                  ).then_inc(onehot_ready if g < GROUPS else mid_onehot_ready, 1)

            def pick(c, g, bank):
                if g == 0:
                    for lane in range(PER_GROUP):
                        dve.wait_ge(slot_in[lane], 16 * (c + 1))
                dve.wait_ge(looked_up, c * GROUPS + g + 1)
                j = C_J8 if GROUP_W[g] == W8 else C_J10
                dve.scalar_tensor_tensor(out=picked[:, g % 2, :], in0=slot_b[:, g, :], scalar=fc[:, j:j + 1],
                                         in1=bank[:, :], op0=ALU.is_equal, op1=ALU.mult).then_inc(picked_ready, 1)

            def pick_middle(c, r):
                dve.wait_ge(mid_looked_up, (c - 1) * (TILES // MID_TILES) + r + 1)
                if r == 0:
                    dve.wait_ge(mid_calc, 3)
                else:
                    dve.wait_ge(mid_ready, ((c - 1) * TILES + r * MID_TILES) * NMID)
                for n in range(MID_TILES):
                    t = r * MID_TILES + n
                    for i in range(NMID):
                        at = n * NMID + i
                        dve.scalar_tensor_tensor(out=mid_picked[:, at, :], in0=slots,
                                                 scalar=mid_slot[:, bass.ds((c * TILES + t) * NMID + i, 1)],
                                                 in1=look[:, at * WMID:(at + 1) * WMID], op0=ALU.is_equal,
                                                 op1=ALU.mult, accum_out=rsum[:, t, NFETCH + i:NFETCH + i + 1]
                                                 ).then_inc(mid_ready, 1)

            def sum_rows(c, t, first):
                n = NL if first else NFETCH
                dve.wait_ge(rows_in[t], rows_landed(c, first))
                dve.tensor_reduce(rsum[:, t, 0:n], rows[:, t, 0:n, :], AX.X, ALU.add).then_inc(rows_summed[t], 1)
                dve.tensor_copy(idx[:, t, :], idc[:, bass.ds(((c + 1) * TILES + t) * NL, NFETCH)]
                                ).then_inc(idx_ready[t], 1)

            def split_rows(c, first):
                for t in range(TILES):
                    dve.wait_ge(rows_summed[t], c + 1)
                if not first:
                    dve.wait_ge(mid_ready, c * TILES * NMID)
                split(rsum[:, :, :], lambda i: rrest[:, i, :, :], lambda i: rparts[:, :, i, :], row_split, 4 * c,
                      rparts_ready)

            def multiply(c, k):
                if not (k == 0 and c is FIRST):
                    dve.wait_ge(z_lo_ready, c * KCH + k)
                dve.wait_ge(factor_ready, c * KCH + k + 1)
                dve.tensor_tensor(z[0:KROWS[k], :], factor[0:KROWS[k], :], pb[0:KROWS[k], :],
                                  ALU.mult).then_inc(z_product, 1)

            def remainder(c, k):
                dve.wait_ge(z_hi_ready, c * KCH + k + 1)
                dve.tensor_tensor(z_lo[0:KROWS[k], k % ZRING, :], z[0:KROWS[k], :],
                                  z_hi[0:KROWS[k], k % ZRING, :].bitcast(F32), ALU.subtract).then_inc(z_lo_ready, 1)

            def sum_group(g):
                w = GROUP_W[g]
                sum_stage(g, PER_GROUP * w, tsum[0:SHELVES, g * PER_GROUP:(g + 1) * PER_GROUP, 0:w])

            def split_groups(n):
                a, b = BATCHES[n]
                w = GROUP_W[a]
                wait_summed(dve, a, b)
                if n == 0:
                    dve.wait_ge(zeroed, 1)
                fa, fb = a * PER_GROUP, b * PER_GROUP
                split(tsum[0:SHELVES, fa:fb, 0:w], lambda i: (trest, tsum)[i][0:SHELVES, fa:fb, 0:w],
                      lambda i: tparts[0:SHELVES, fa:fb, i * w:(i + 1) * w], table_split, 4 * n, tparts_ready)

            for g in (0, 1, 2):
                sum_group(g)
                onehots(FIRST, g)
            split_groups(0)
            for g in (3, 4):
                onehots(FIRST, g)
            for g in (0, 1):
                pick(0, g, FIRST_BANKS[g % 2])
            sum_group(3)
            pick(0, 2, FIRST_BANKS[0])
            onehots(FIRST, 5)
            sum_group(4)
            split_groups(1)
            onehots(FIRST, 6)
            sum_group(5)
            for g in (3, 4):
                pick(0, g, FIRST_BANKS[g % 2])
            sum_group(6)
            split_groups(2)
            for g in (5, 6):
                pick(0, g, FIRST_BANKS[g % 2])

            def split_w1(k):
                dve.wait_ge(w1_rounded, k + 1)
                dve.tensor_tensor(w1_lo[0:KROWS[k], k, :], w1_raw[k][0:KROWS[k], :],
                                  w1_hi[0:KROWS[k], k, :].bitcast(F32), ALU.subtract).then_inc(w1_split, 1)

            split_w1(0)
            sum_rows(0, 0, True)
            multiply(FIRST, 0)
            split_w1(1)
            remainder(0, 0)
            sum_rows(0, 1, True)
            multiply(0, 1)
            split_w1(2)
            remainder(0, 1)

            def sum_middle(n):
                i, q = divmod(n, PIECES)
                sum_stage(PIECE_USE + n, PIECE, msum[0:SHELVES, i, q * PIECE:(q + 1) * PIECE])
                if q == PIECES - 1:
                    wait_summed(dve, PIECE_USE + i * PIECES, PIECE_USE + n + 1)
                    split(msum[0:SHELVES, i, :], lambda n: (mrest, msum)[n][0:SHELVES, i, :],
                          lambda n: mparts[0:SHELVES, i, n, :], mid_split, 4 * i, mparts_ready)

            def step(c, first=False, last=False):
                if not first:
                    multiply(c, 1)
                    for g in range(0 if last else HOT_START):
                        onehots(c + 1, g)
                    remainder(c, 1)
                for k in range(KCH):
                    for m in range(M1):
                        at = k * M1 + m
                        if not last:
                            for g, hot_step in (HOT_STEPS_FIRST if first else HOT_STEPS).items():
                                if at == hot_step:
                                    onehots(c + 1, g)
                            if at in GROUP_STEPS:
                                pick(c + 1, GROUP_STEPS.index(at), look)
                            if at == MID_HOT_STEP:
                                onehots(c + 1, GROUPS)
                        if m == 1 and 0 < k < KCH - 1:
                            remainder(c, k + 1)
                        for t, row_step in ROW_STEPS.items():
                            if at == row_step:
                                sum_rows(c, t, first)
                        if at == NEXT_ROW_STEP and not last:
                            sum_rows(c + 1, 0, False)
                        if first and at == 2:
                            split_w1(5)
                        if at in MID_STEPS and not first:
                            pick_middle(c, MID_STEPS.index(at))
                        if first and at in (1, 2):
                            split_w1(at + 2)
                        if at == max(ROW_STEPS.values()):
                            split_rows(c, first)
                        if first and at in PIECE_STEPS:
                            sum_middle(PIECE_STEPS.index(at))
                    if k < 4:
                        multiply(c, k + 2)
                    if first and k == 0:
                        dve.wait_ge(w2_rounded, 1)
                        dve.tensor_tensor(w2_lo[:, :, :], w2_raw[:, :, :], w2_hi[:, :, :].bitcast(F32),
                                          ALU.subtract).then_inc(w2_split, 1)
                for m in range(M1):
                    dve.wait_ge(h1_hi_ready, c * M1 + m + 1)
                    dve.scalar_tensor_tensor(out=h1_lo[:, m, :], in0=ph[m][:, :], scalar=0.0,
                                             in1=h1_hi[:, m, :].bitcast(F32), op0=ALU.max, op1=ALU.subtract
                                             ).then_inc(h1_lo_ready, 1)
                if not last:
                    multiply(c + 1, 0)
                    remainder(c + 1, 0)
                    sum_rows(c + 1, 1, False)
                for n in range(len(PIECE_STEPS), NMID * PIECES if first else 0):
                    sum_middle(n)

            step(0, first=True)
            with dve.Fori(1, CHUNKS - 1) as c:
                step(c)
            step(CHUNKS - 1, last=True)

        @block.scalar
        def _(act):
            act.dma_start(bc[:, O_ID:], bconst[:, O_ID:]).then_inc(bconst_in, 16)
            act.dma_start(dense[:, :], dense_t[:, 0:CHUNK]).then_inc(dense_in, 16)
            act.dma_start(cols[:, :], columns).then_inc(columns_in, 16)
            for f in range(NE):
                act.wait_ge(shelf_spread, f + 1)
                act.copy(shelf_b[:, f, :], SPREAD_BANKS[f % 3][:, :]).then_inc(shelf_copied, 1)

            def round_w1(k):
                act.wait_ge(w1_in[k], 32)
                act.copy(w1_hi[0:KROWS[k], k, :], w1_raw[k][0:KROWS[k], :]).then_inc(w1_rounded, 1)

            round_w1(0)
            round_w1(1)

            def round_z(c, k, last=False):
                act.wait_ge(selected, c * KCH + k + 1)
                act.copy(factor[0:KROWS[k], :], pa[0:KROWS[k], :]).then_inc(factor_ready, 1)
                act.wait_ge(z_product, c * KCH + k + 1)
                if k == KCH - 1:
                    act.wait_ge(dense_in, 16 * (c + 1))
                    act.copy(z[0:APPENDED, :], dense[:, :]).then_inc(dense_placed, 1)
                    act.wait_ge(dense_placed, c + 1)
                    if not last:
                        act.dma_start(dense[:, :], dense_t[:, bass.ds((c + 1) * CHUNK, CHUNK)]).then_inc(dense_in, 16)
                act.copy(z_hi[0:KROWS[k], k % ZRING, :], z[0:KROWS[k], :]).then_inc(z_hi_ready, 1)

            act.wait_ge(early_acc, 1)
            act.copy(s_early[:, :], early[0:RE, :]).then_inc(early_ready, 1)
            act.wait_ge(columns_in, 16)
            round_z(0, 0)
            round_w1(2)
            round_z(0, 1)
            for k in range(3, KCH):
                round_w1(k)
            act.wait_ge(w2_in, 16)
            act.copy(w2_hi[:, :, :], w2_raw[:, :, :]).then_inc(w2_rounded, 1)

            def step(c, first=False, last=False):
                for k in range(KCH):
                    if k == 1:
                        act.wait_ge(late_acc, c + 1)
                        act.copy(s_late[:, :], look[0:RL, :]).then_inc(late_ready, 1)
                    if k < 4:
                        round_z(c, k + 2, last)
                for m in range(M1):
                    if m == M2 and not last:
                        act.wait_ge(early_acc, c + 2)
                        act.copy(s_early[:, :], early[0:RE, :]).then_inc(early_ready, 1)
                    act.wait_ge(h1_acc, c * M1 + m + 1)
                    act.activation(h1_hi[:, m, :], ph[m][:, :], ACT.Relu).then_inc(h1_hi_ready, 1)
                if not last:
                    round_z(c + 1, 0)
                for m in range(M2):
                    act.wait_ge(h2_acc, c * M2 + m + 1)
                    act.activation(h2[:, m, :], ph[m][:, :], ACT.Relu, bias=b2_sb[:, m:m + 1]).then_inc(h2_ready, 1)
                if not last:
                    round_z(c + 1, 1)
                act.wait_ge(y_acc, c + 1)
                if first:
                    act.wait_ge(scratch_shelf, 16)
                    act.wait_ge(scratch_slot, 16)
                if not first:
                    act.wait_ge(y_out, 16 * c)
                act.copy(y_sb[:, :], ph[2][0:1, :]).then_inc(y_ready, 1)
                act.wait_ge(y_ready, c + 1)
                act.dma_start(out[:, bass.ds(c * CHUNK, CHUNK)], y_sb[:, :]).then_inc(y_out, 16)

            step(0, first=True)
            with act.Fori(1, CHUNKS - 1) as c:
                step(c)
            step(CHUNKS - 1, last=True)
            act.wait_ge(y_out, 16 * CHUNKS)

        @block.tensor
        def _(pe):
            pe.wait_ge(bconst_in, 16)

            def lookup(c, g, bank):
                pe.wait_ge(onehot_ready, c * GROUPS + g + 1)
                for lane in range(PER_GROUP):
                    f = g * PER_GROUP + lane
                    mm = pe.matmul(bank[lane * LANE:(lane + 1) * LANE, :], tparts[0:SHELVES, f, :],
                                   onehot[0:SHELVES, f, :], start=True, stop=True)
                mm.then_inc(looked_up, 1)

            def sum_lanes(c, g):
                pe.wait_ge(picked_ready, c * GROUPS + g + 1)
                mm = pe.matmul(early[0:RE, :], sum_w[:, g, :], picked[:, g % 2, :], start=(g == 0),
                               stop=(g == GROUPS - 1))
                if g == GROUPS - 1:
                    mm.then_inc(early_acc, 1)

            def lookup_middle(c, r):
                if r == 0:
                    pe.wait_ge(mid_onehot_ready, c)
                    pe.wait_ge(mparts_ready, NMID)
                else:
                    pe.wait_ge(mid_ready, ((c - 1) * TILES + r * MID_TILES) * NMID)
                for n in range(MID_TILES):
                    t = r * MID_TILES + n
                    for i in range(NMID):
                        a = (n * NMID + i) * WMID
                        for part in range(PARTS):
                            mm = pe.matmul(look[:, a:a + WMID], onehot[0:SHELVES, NE + i, t * P:(t + 1) * P],
                                           mparts[0:SHELVES, i, part, :], start=(part == 0), stop=(part == PARTS - 1))
                mm.then_inc(mid_looked_up, 1)

            def transpose_late(c, first):
                pe.wait_ge(rparts_ready, c + 1)
                if not first:
                    pe.wait_ge(mid_ready, c * TILES * NMID)
                for t in range(TILES):
                    mm = pe.matmul(look[0:RL, t * P:(t + 1) * P], rparts[:, t, :, :].rearrange("p a f -> p (a f)"),
                                   ident, start=True, stop=True)
                mm.then_inc(late_acc, 1)

            def select(c, k):
                n = KROWS[k]

                def pick_rows(bank, o_early=None, o_late=None):
                    if o_early is not None:
                        mm = pe.matmul(bank[0:n, :], bc[0:RE, o_early:o_early + n], s_early[:, :],
                                       start=True, stop=o_late is None)
                    if o_late is not None:
                        mm = pe.matmul(bank[0:n, :], bc[0:RL, o_late:o_late + n], s_late[:, :],
                                       start=o_early is None, stop=True)
                    return mm

                if k == 0:
                    pe.wait_ge(early_ready, c + 1)
                if k == 3:
                    pe.wait_ge(late_ready, c + 1)
                if not (k == 0 and c is FIRST):
                    pe.wait_ge(z_product, c * KCH + k)
                pick_rows(pa, O_E1 + k * P, O_L1 if k == 5 else None)
                if k < 3:
                    pick_rows(pb, O_E2 + k * P).then_inc(selected, 1)
                else:
                    pick_rows(pb, None, O_L2 + (k - 3) * P).then_inc(selected, 1)

            pe.wait_ge(shelf_ready, 1)
            for f in range(NE):
                if f >= 3:
                    pe.wait_ge(shelf_copied, f - 2)
                pe.matmul(SPREAD_BANKS[f % 3][:, :], ident[0:QR_ROWS, f:f + 1].to_broadcast([QR_ROWS, P]),
                          shelf_h[:, :], start=True, stop=True).then_inc(shelf_spread, 1)
            pe.wait_ge(select_in, 16)
            for a, b in BATCHES:
                for g in range(a, b):
                    pe.wait_ge(tparts_ready, BATCHES.index((a, b)) + 1)
                    if g >= 2:
                        pe.wait_ge(picked_ready, g - 1)
                    lookup(0, g, FIRST_BANKS[g % 2])
                    if g > 0:
                        sum_lanes(0, g - 1)
            sum_lanes(0, GROUPS - 1)
            select(FIRST, 0)
            select(0, 1)

            def step(c, first=False, last=False):
                for k in range(KCH):
                    pe.wait_ge(z_hi_ready, c * KCH + k + 1)
                    if first:
                        pe.wait_ge(w1_split, k + 1)
                    n = KROWS[k]
                    for m in range(M1):
                        if k == 0 and m == 2 and not first:
                            pe.wait_ge(y_ready, c)
                        hi, lo = w1_hi[0:n, k, m * P:(m + 1) * P], w1_lo[0:n, k, m * P:(m + 1) * P]
                        pe.matmul(ph[m][:, :], hi, z_hi[0:n, k % ZRING, :], start=(k == 0), stop=False)
                        pe.matmul(ph[m][:, :], lo, z_hi[0:n, k % ZRING, :], start=False, stop=False)
                        if m == 0:
                            pe.wait_ge(z_lo_ready, c * KCH + k + 1)
                        mm = pe.matmul(ph[m][:, :], hi, z_lo[0:n, k % ZRING, :], start=False, stop=(k == KCH - 1))
                        if k == KCH - 1:
                            mm.then_inc(h1_acc, 1)
                        at = k * M1 + m
                        if not last and at in GROUP_STEPS:
                            g = GROUP_STEPS.index(at)
                            if g > 0:
                                pe.wait_ge(picked_ready, (c + 1) * GROUPS + g)
                            else:
                                pe.wait_ge(late_ready, c + 1)
                            lookup(c + 1, g, look)
                        if not last and at in SUM_STEPS:
                            sum_lanes(c + 1, SUM_STEPS.index(at))
                        if not first and at in MID_STEPS:
                            lookup_middle(c, MID_STEPS.index(at))
                        if at == LATE_STEP:
                            transpose_late(c, first)
                    if k < 4:
                        select(c, k + 2)
                if first:
                    pe.wait_ge(w2_split, 1)
                for k in range(M1):
                    pe.wait_ge(h1_hi_ready, c * M1 + k + 1)
                    if k == 0:
                        pe.wait_ge(h1_lo_ready, c * M1 + M2)
                    for m in range(M2):
                        hi, lo = w2_hi[:, k, m * P:(m + 1) * P], w2_lo[:, k, m * P:(m + 1) * P]
                        pe.matmul(ph[m][:, :], hi, h1_hi[:, k, :], start=(k == 0), stop=False)
                        pe.matmul(ph[m][:, :], lo, h1_hi[:, k, :], start=False, stop=False)
                        if m == 0:
                            pe.wait_ge(h1_lo_ready, c * M1 + k + 1)
                        mm = pe.matmul(ph[m][:, :], hi, h1_lo[:, k, :], start=False, stop=(k == M1 - 1))
                        if k == M1 - 1:
                            mm.then_inc(h2_acc, 1)
                    if k in (0, M1 - 1) and not last:
                        select(c + 1, k // (M1 - 1))
                for m in range(M2):
                    pe.wait_ge(h2_ready, c * M2 + m + 1)
                    mm = pe.matmul(ph[2][0:1, :], w3_sb[:, m:m + 1], h2[:, m, :], start=(m == 0),
                                   stop=(m == M2 - 1))
                mm.then_inc(y_acc, 1)

            step(0, first=True)
            with pe.Fori(1, CHUNKS - 1) as c:
                step(c)
            step(CHUNKS - 1, last=True)


def _pairs():
    early = [(a, b) for a in range(NE) for b in range(a + 1, NE)]
    late = [(a, b) for a in range(NE) for b in range(NE, FIELDS)]
    late += [(a, b) for a in range(NE, FIELDS) for b in range(a + 1, FIELDS)]
    late[2 * P:2 * P] = [None] * APPENDED
    return [early[0:P], early[P:2 * P], early[2 * P:], late[0:P], late[P:2 * P], late[2 * P:]]


def _w1_rows(np):
    index = {pair: n for n, pair in enumerate(zip(*(x.tolist() for x in np.triu_indices(FIELDS, k=1))))}
    rows, dense = [], PAIRS
    for chunk in _pairs():
        for pair in chunk:
            if pair is None:
                rows.append(dense)
                dense += 1
            else:
                rows.append(index[tuple(sorted((ORDER[pair[0]], ORDER[pair[1]])))])
    return np.array(rows)


def _shape_constants(np):
    fconst = np.zeros((P, 6), np.float32)
    p = np.arange(P)
    fconst[:, C_PART] = p
    for col, w in ((C_J8, W8), (C_J10, W10)):
        r = p % LANE
        fconst[:, col] = np.where(r < PARTS * w, r % w, -1)
    for row in range(QR_ROWS):
        f = row % NHOT
        w = VOCAB[ORDER[f]] // SHELVES if f < NE else WMID
        fconst[row, C_INV] = 1.0 / w
        fconst[row, C_OFF] = 0.5 / w - 0.5
        fconst[row, C_NEGW] = -w
    bconst = np.zeros((P, NCONST), np.float32)
    for g in range(GROUPS):
        w = GROUP_W[g]
        for lane in range(PER_GROUP):
            for i in range(PARTS):
                a = lane * LANE + i * w
                bconst[a:a + w, O_SUM + g * RE + i * NE + g * PER_GROUP + lane] = 1
    for k, chunk in enumerate(_pairs()):
        for r, pair in enumerate(chunk):
            for place, o_early, o_late in zip(pair or (), (O_E1 + k * P, O_E2 + k * P), (O_L1, O_L2 + (k - 3) * P)):
                for i in range(PARTS):
                    if place < NE:
                        bconst[i * NE + place, o_early + r] = 1
                    else:
                        bconst[i * NL + place - NE, o_late + r] = 1
    bconst[p, O_ID + p] = 1
    bconst[:, O_SLOT:] = np.arange(WMID)
    return fconst, bconst


def kernel(**inputs):
    import numpy as np
    import concourse.bacc as bacc
    from concourse.bass_utils import run_bass_kernel_spmd

    nc = bacc.Bacc("TRN2", target_bir_lowering=False, num_devices=1)
    arrays = {}

    def dram(name, a):
        a = np.ascontiguousarray(a)
        arrays[name] = a
        return nc.dram_tensor(name, a.shape, mybir.dt.from_np(a.dtype), kind="ExternalInput").ap()

    ids = np.asarray(inputs["ids"])
    hot = np.array(EARLY + LATE[NFETCH:])
    by_field = ids.T[hot].reshape(NHOT, CHUNKS, CHUNK).transpose(1, 0, 2).reshape(QR_ROWS, CHUNK)
    by_row = ids[:, np.array(LATE)].reshape(BATCH // P, P, NL).transpose(1, 0, 2).reshape(P, -1)
    by_row = np.concatenate([by_row, np.zeros((P, TILES * NL), by_row.dtype)], axis=1)

    def shelves(fields):
        return np.concatenate([np.asarray(inputs[f"tbl_{f}"]).reshape(SHELVES, -1) for f in fields], axis=1)

    columns = np.concatenate([np.asarray(inputs[n]).reshape(-1, P).T for n in ("W_top3", "b_top2")], axis=1)
    w1 = np.concatenate([np.asarray(inputs["W_top1"]), np.asarray(inputs["b_top1"]).reshape(1, -1)])
    dense = np.asarray(inputs["dense_ctx"])
    dense_t = np.concatenate([dense.T, np.ones((1, BATCH), dense.dtype)])
    fconst, bconst = _shape_constants(np)
    out = nc.dram_tensor("out", (1, BATCH), F32, kind="ExternalOutput").ap()
    build_tower(
        nc, dram("ids_rows", by_field), dram("ids_cols", by_row), dram("dense_t", dense_t),
        dram("tab8", shelves(F8)), dram("tab10", shelves(F10)), [dram(f"tab_{f}", inputs[f"tbl_{f}"]) for f in LATE],
        dram("w1", w1[_w1_rows(np)]), dram("w2", inputs["W_top2"]),
        dram("columns", columns), dram("fconst", fconst), dram("bconst", bconst.astype(np.dtype("bfloat16"))), out)
    r = run_bass_kernel_spmd(nc, [arrays], core_ids=[0])
    return r.results[0]["out"].reshape(BATCH, 1)
```
